# Optimizing a Trainium2 kernel written in Bass

```python
import numpy as np
import jax
import jax.numpy as jnp

def _softmax(x, axis=-1):
    return jax.nn.softmax(x, axis=axis)

def _gelu(x):
    return jax.nn.gelu(x, approximate=True)

def _silu(x):
    return jax.nn.silu(x)

def _sigmoid(x):
    return jax.nn.sigmoid(x)

def _layernorm(x, axis=-1, eps=1e-05):
    m = jnp.mean(x, axis=axis, keepdims=True)
    v = jnp.var(x, axis=axis, keepdims=True)
    return (x - m) / jnp.sqrt(v + eps)

def _scatter_add(tgt, idx, src, axis=0):
    return tgt.at[idx].add(src)

def _segment_sum(src, seg, n):
    return jax.ops.segment_sum(src, seg, n)
kernel_name = 'mk_seq_preln_d2_jaxref_r8_ba61b9'

def setup_inputs(seed: int=0):
    np.random.seed(seed)
    _w = jnp.asarray

    def _L0_attn_setup():
        import jax, jax.numpy as jnp
        import numpy as np
        NUM_HEADS = 16

        def rotate_half(x):
            h = x.shape[-1] // 2
            return jnp.concatenate([-x[..., h:], x[..., :h]], axis=-1)
        key = jax.random.key(seed)
        ks = jax.random.split(key, 9)
        d = 128
        s = 0.02
        return {'x': jax.random.normal(ks[0], (4, 256, d), dtype=jnp.float32), 'wq': jax.random.normal(ks[1], (d, d), dtype=jnp.float32) * s, 'bq': jax.random.normal(ks[2], (d,), dtype=jnp.float32) * s, 'wk': jax.random.normal(ks[3], (d, d), dtype=jnp.float32) * s, 'bk': jax.random.normal(ks[4], (d,), dtype=jnp.float32) * s, 'wv': jax.random.normal(ks[5], (d, d), dtype=jnp.float32) * s, 'bv': jax.random.normal(ks[6], (d,), dtype=jnp.float32) * s, 'wo': jax.random.normal(ks[7], (d, d), dtype=jnp.float32) * s, 'bo': jax.random.normal(ks[8], (d,), dtype=jnp.float32) * s}
    _L0_attn_in = _L0_attn_setup()

    def _L0_ffn_setup():
        import jax, jax.numpy as jnp
        import numpy as np
        DIM = 128
        DEPTH = 6
        HEADS = 16
        DIM_HEAD = 64
        WINDOW = 32
        INNER = HEADS * DIM_HEAD
        DIM_INNER = int(DIM * 4 * 2 / 3)
        QK_SCALE = 8.0

        def shift_tokens(t):
            a, s = jnp.split(t, 2, -1)
            s = jnp.pad(s, ((0, 0), (1, 0), (0, 0)))[:, :-1]
            return jnp.concatenate([a, s], -1)

        def l2norm(t):
            return t / jnp.maximum(jnp.linalg.norm(t, axis=-1, keepdims=True), 1e-12)

        def rotate_half(x):
            x1, x2 = jnp.split(x, 2, -1)
            return jnp.concatenate([-x2, x1], -1)

        def rotary_tables(n):
            half = jnp.arange(0, DIM_HEAD, 2, dtype=jnp.float32)
            inv_freq = 1.0 / 10000.0 ** (half / DIM_HEAD)
            t = jnp.arange(n, dtype=jnp.float32)
            freqs = t[:, None] * inv_freq[None, :]
            freqs = jnp.concatenate([freqs, freqs], -1)
            base_scale = (half + 0.4 * DIM_HEAD) / (1.4 * DIM_HEAD)
            power = (t - n // 2) / (WINDOW // 2)
            scale = base_scale[None, :] ** power[:, None]
            scale = jnp.concatenate([scale, scale], -1)
            return (freqs, scale)

        def local_attention(q, k, v):
            b, h, n, d = q.shape
            w = WINDOW
            nw = n // w
            bq = q.reshape(b, h, nw, w, d)
            bk = k.reshape(b, h, nw, w, d)
            bv = v.reshape(b, h, nw, w, d)

            def look(t):
                p = jnp.pad(t, ((0, 0), (0, 0), (1, 0), (0, 0), (0, 0)))
                return jnp.concatenate([p[:, :, :nw], p[:, :, 1:]], axis=3)
            bk2, bv2 = (look(bk), look(bv))
            seq = jnp.arange(n).reshape(nw, w)
            seq_p = jnp.pad(seq, ((1, 0), (0, 0)), constant_values=-1)
            jt = jnp.concatenate([seq_p[:nw], seq_p[1:]], axis=1)
            it = seq[:, :, None]
            jb = jt[:, None, :]
            mask = (it < jb) | (it > jb + w) | (jb == -1)
            sim = jnp.einsum('bhwie,bhwje->bhwij', bq, bk2) * QK_SCALE
            sim = jnp.where(mask, -jnp.finfo(sim.dtype).max, sim)
            attn = jax.nn.softmax(sim, -1)
            out = jnp.einsum('bhwij,bhwje->bhwie', attn, bv2)
            return out.reshape(b, h, n, d)

        def attn_layer(x, Wqkv, qs, ksc, Wo):
            b, n, _ = x.shape
            qkv = x @ Wqkv
            q, k, v = jnp.split(qkv, 3, -1)
            sh = lambda t: t.reshape(b, n, HEADS, DIM_HEAD).transpose(0, 2, 1, 3)
            q, k, v = (sh(q), sh(k), sh(v))
            q = l2norm(q) * qs
            k = l2norm(k) * ksc
            freqs, scale = rotary_tables(n)
            cos, sin = (jnp.cos(freqs), jnp.sin(freqs))
            q = q * cos * scale + rotate_half(q) * sin * scale
            inv = 1.0 / scale
            k = k * cos * inv + rotate_half(k) * sin * inv
            out = local_attention(q, k, v)
            out = out.transpose(0, 2, 1, 3).reshape(b, n, INNER)
            return out @ Wo

        def ffn_layer(x, g, bln, W1, b1, W2, b2):
            mu = x.mean(-1, keepdims=True)
            var = ((x - mu) ** 2).mean(-1, keepdims=True)
            xn = (x - mu) / jnp.sqrt(var + 1e-05) * g + bln
            hg = xn @ W1 + b1
            a, gate = jnp.split(hg, 2, -1)
            return a * jax.nn.gelu(gate, approximate=False) @ W2 + b2
        key = jax.random.key(seed)
        ks = jax.random.split(key, 8)
        B, N = (2, 256)
        init = lambda k, shape: jax.random.normal(k, shape, jnp.float32) * 0.02
        return {'x': jax.random.normal(ks[0], (B, N, DIM), jnp.float32), 'Wqkv': init(ks[1], (DEPTH, DIM, 3 * INNER)), 'q_scale': jnp.ones((DEPTH, DIM_HEAD), jnp.float32), 'k_scale': jnp.ones((DEPTH, DIM_HEAD), jnp.float32), 'Wo': init(ks[2], (DEPTH, INNER, DIM)), 'ln_g': jnp.ones((DEPTH, DIM), jnp.float32), 'ln_b': jnp.zeros((DEPTH, DIM), jnp.float32), 'W1': init(ks[3], (DEPTH, DIM, 2 * DIM_INNER)), 'b1': jnp.zeros((DEPTH, 2 * DIM_INNER), jnp.float32), 'W2': init(ks[4], (DEPTH, DIM_INNER, DIM)), 'b2': jnp.zeros((DEPTH, DIM), jnp.float32)}
    _L0_ffn_in = _L0_ffn_setup()

    def _L1_attn_setup():
        import jax, jax.numpy as jnp
        import numpy as np
        NUM_HEADS = 16
        D_MODEL = 128
        D_K = D_MODEL // NUM_HEADS
        MAX_SEQ_LEN = 512
        ROPE_BASE = 10000.0
        BATCH = 2
        SEQ_LEN = 256

        def _rope_tables(seq_len, d_k, base=ROPE_BASE):
            theta = 1.0 / base ** (jnp.arange(0, d_k, 2, dtype=jnp.float32) / d_k)
            m = jnp.arange(seq_len, dtype=jnp.float32)
            m_theta = jnp.outer(m, theta)
            ang = jnp.concatenate([m_theta, m_theta], axis=-1)
            return (jnp.cos(ang), jnp.sin(ang))

        def _apply_rope(x, cos, sin):
            d2 = x.shape[-1] // 2
            x1, x2 = (x[..., :d2], x[..., d2:])
            x_flip = jnp.concatenate([-x2, x1], axis=-1)
            return x * cos + x_flip * sin
        key = jax.random.key(seed)
        kx, kq, kk, kv, ko = jax.random.split(key, 5)
        s = 1.0 / np.sqrt(D_MODEL)
        x = jax.random.normal(kx, (BATCH, SEQ_LEN, D_MODEL), dtype=jnp.float32)
        W_Q = jax.random.uniform(kq, (D_MODEL, D_MODEL), jnp.float32, -s, s)
        W_K = jax.random.uniform(kk, (D_MODEL, D_MODEL), jnp.float32, -s, s)
        W_V = jax.random.uniform(kv, (D_MODEL, D_MODEL), jnp.float32, -s, s)
        W_O = jax.random.uniform(ko, (D_MODEL, D_MODEL), jnp.float32, -s, s)
        return {'x': x, 'W_Q': W_Q, 'W_K': W_K, 'W_V': W_V, 'W_O': W_O}
    _L1_attn_in = _L1_attn_setup()

    def _L1_ffn_setup():
        import jax, jax.numpy as jnp
        import numpy as np
        D_MODEL = 128
        NUM_HEADS = 4
        NUM_EXPERTS = 8
        TOP_K = 2
        D_FF = 128
        EPS = 1e-06

        def _rmsnorm(x, g):
            return x * jax.lax.rsqrt(jnp.mean(x * x, axis=-1, keepdims=True) + EPS) * g

        def _swiglu(x, w1, w2, w3):
            return jax.nn.silu(x @ w1.T) * (x @ w3.T) @ w2.T
        key = jax.random.key(seed)
        ks = jax.random.split(key, 16)
        d, e, f = (D_MODEL, NUM_EXPERTS, D_FF)
        dc = d // 4
        s = 0.02
        return {'X': jax.random.normal(ks[0], (2, 128, d), dtype=jnp.float32), 'g1': jnp.ones((d,), jnp.float32), 'g2': jnp.ones((d,), jnp.float32), 'Wq': jax.random.normal(ks[1], (d, d), jnp.float32) * s, 'Wkc': jax.random.normal(ks[2], (dc, d), jnp.float32) * s, 'Wvc': jax.random.normal(ks[3], (dc, d), jnp.float32) * s, 'Wo': jax.random.normal(ks[4], (d, d), jnp.float32) * s, 'Wr': jax.random.normal(ks[5], (e, d), jnp.float32) * s, 'expert_bias': jnp.zeros((e,), jnp.float32), 'sW1': jax.random.normal(ks[6], (f, d), jnp.float32) * s, 'sW2': jax.random.normal(ks[7], (d, f), jnp.float32) * s, 'sW3': jax.random.normal(ks[8], (f, d), jnp.float32) * s, 'eW1': jax.random.normal(ks[9], (e, f, d), jnp.float32) * s, 'eW2': jax.random.normal(ks[10], (e, d, f), jnp.float32) * s, 'eW3': jax.random.normal(ks[11], (e, f, d), jnp.float32) * s}
    _L1_ffn_in = _L1_ffn_setup()
    _d = {'L0_attn_x': _L0_attn_in['x'], 'L0_attn_wq': _L0_attn_in['wq'], 'L0_attn_bq': _L0_attn_in['bq'], 'L0_attn_wk': _L0_attn_in['wk'], 'L0_attn_bk': _L0_attn_in['bk'], 'L0_attn_wv': _L0_attn_in['wv'], 'L0_attn_bv': _L0_attn_in['bv'], 'L0_attn_wo': _L0_attn_in['wo'], 'L0_attn_bo': _L0_attn_in['bo'], 'L0_ffn_Wqkv': _L0_ffn_in['Wqkv'], 'L0_ffn_q_scale': _L0_ffn_in['q_scale'], 'L0_ffn_k_scale': _L0_ffn_in['k_scale'], 'L0_ffn_Wo': _L0_ffn_in['Wo'], 'L0_ffn_ln_g': _L0_ffn_in['ln_g'], 'L0_ffn_ln_b': _L0_ffn_in['ln_b'], 'L0_ffn_W1': _L0_ffn_in['W1'], 'L0_ffn_b1': _L0_ffn_in['b1'], 'L0_ffn_W2': _L0_ffn_in['W2'], 'L0_ffn_b2': _L0_ffn_in['b2'], 'L1_attn_W_Q': _L1_attn_in['W_Q'], 'L1_attn_W_K': _L1_attn_in['W_K'], 'L1_attn_W_V': _L1_attn_in['W_V'], 'L1_attn_W_O': _L1_attn_in['W_O'], 'L1_ffn_g1': _L1_ffn_in['g1'], 'L1_ffn_g2': _L1_ffn_in['g2'], 'L1_ffn_Wq': _L1_ffn_in['Wq'], 'L1_ffn_Wkc': _L1_ffn_in['Wkc'], 'L1_ffn_Wvc': _L1_ffn_in['Wvc'], 'L1_ffn_Wo': _L1_ffn_in['Wo'], 'L1_ffn_Wr': _L1_ffn_in['Wr'], 'L1_ffn_expert_bias': _L1_ffn_in['expert_bias'], 'L1_ffn_sW1': _L1_ffn_in['sW1'], 'L1_ffn_sW2': _L1_ffn_in['sW2'], 'L1_ffn_sW3': _L1_ffn_in['sW3'], 'L1_ffn_eW1': _L1_ffn_in['eW1'], 'L1_ffn_eW2': _L1_ffn_in['eW2'], 'L1_ffn_eW3': _L1_ffn_in['eW3']}
    _x0 = _d['L0_attn_x']
    _d['L0_attn_x'] = jax.random.normal(jax.random.fold_in(jax.random.key(seed), 1), (4, 1024, 128), dtype=_x0.dtype)
    del _x0
    return _d

def reference(L0_attn_x, L0_attn_wq, L0_attn_bq, L0_attn_wk, L0_attn_bk, L0_attn_wv, L0_attn_bv, L0_attn_wo, L0_attn_bo, L0_ffn_Wqkv, L0_ffn_q_scale, L0_ffn_k_scale, L0_ffn_Wo, L0_ffn_ln_g, L0_ffn_ln_b, L0_ffn_W1, L0_ffn_b1, L0_ffn_W2, L0_ffn_b2, L1_attn_W_Q, L1_attn_W_K, L1_attn_W_V, L1_attn_W_O, L1_ffn_g1, L1_ffn_g2, L1_ffn_Wq, L1_ffn_Wkc, L1_ffn_Wvc, L1_ffn_Wo, L1_ffn_Wr, L1_ffn_expert_bias, L1_ffn_sW1, L1_ffn_sW2, L1_ffn_sW3, L1_ffn_eW1, L1_ffn_eW2, L1_ffn_eW3):

    def _L0_attn_ref(x, wq, bq, wk, bk, wv, bv, wo, bo):
        import jax, jax.numpy as jnp
        import numpy as np
        NUM_HEADS = 16

        def rotate_half(x):
            h = x.shape[-1] // 2
            return jnp.concatenate([-x[..., h:], x[..., :h]], axis=-1)
        b, s, d = x.shape
        h = NUM_HEADS
        hd = d // h
        q = x @ wq.T + bq
        k = x @ wk.T + bk
        v = x @ wv.T + bv
        q = q.reshape(b, s, h, hd).transpose(0, 2, 1, 3)
        k = k.reshape(b, s, h, hd).transpose(0, 2, 1, 3)
        v = v.reshape(b, s, h, hd).transpose(0, 2, 1, 3)
        theta = 10000.0 ** (-2.0 * jnp.arange(hd // 2, dtype=jnp.float32) / hd)
        freqs = jnp.arange(s, dtype=jnp.float32)[:, None] * theta[None, :]
        cos = jnp.repeat(jnp.cos(freqs), 2, axis=-1)[None, None]
        sin = jnp.repeat(jnp.sin(freqs), 2, axis=-1)[None, None]
        q = q * cos + rotate_half(q) * sin
        k = k * cos + rotate_half(k) * sin
        scores = jnp.einsum('bhqd,bhkd->bhqk', q, k) / jnp.sqrt(jnp.float32(hd))
        attn = jax.nn.softmax(scores, axis=-1)
        out = jnp.einsum('bhqk,bhkd->bhqd', attn, v)
        out = out.transpose(0, 2, 1, 3).reshape(b, s, d)
        return out @ wo.T + bo

    def _L0_ffn_ref(x, Wqkv, q_scale, k_scale, Wo, ln_g, ln_b, W1, b1, W2, b2):
        import jax, jax.numpy as jnp
        import numpy as np
        DIM = 128
        DEPTH = 6
        HEADS = 16
        DIM_HEAD = 64
        WINDOW = 32
        INNER = HEADS * DIM_HEAD
        DIM_INNER = int(DIM * 4 * 2 / 3)
        QK_SCALE = 8.0

        def shift_tokens(t):
            a, s = jnp.split(t, 2, -1)
            s = jnp.pad(s, ((0, 0), (1, 0), (0, 0)))[:, :-1]
            return jnp.concatenate([a, s], -1)

        def l2norm(t):
            return t / jnp.maximum(jnp.linalg.norm(t, axis=-1, keepdims=True), 1e-12)

        def rotate_half(x):
            x1, x2 = jnp.split(x, 2, -1)
            return jnp.concatenate([-x2, x1], -1)

        def rotary_tables(n):
            half = jnp.arange(0, DIM_HEAD, 2, dtype=jnp.float32)
            inv_freq = 1.0 / 10000.0 ** (half / DIM_HEAD)
            t = jnp.arange(n, dtype=jnp.float32)
            freqs = t[:, None] * inv_freq[None, :]
            freqs = jnp.concatenate([freqs, freqs], -1)
            base_scale = (half + 0.4 * DIM_HEAD) / (1.4 * DIM_HEAD)
            power = (t - n // 2) / (WINDOW // 2)
            scale = base_scale[None, :] ** power[:, None]
            scale = jnp.concatenate([scale, scale], -1)
            return (freqs, scale)

        def local_attention(q, k, v):
            b, h, n, d = q.shape
            w = WINDOW
            nw = n // w
            bq = q.reshape(b, h, nw, w, d)
            bk = k.reshape(b, h, nw, w, d)
            bv = v.reshape(b, h, nw, w, d)

            def look(t):
                p = jnp.pad(t, ((0, 0), (0, 0), (1, 0), (0, 0), (0, 0)))
                return jnp.concatenate([p[:, :, :nw], p[:, :, 1:]], axis=3)
            bk2, bv2 = (look(bk), look(bv))
            seq = jnp.arange(n).reshape(nw, w)
            seq_p = jnp.pad(seq, ((1, 0), (0, 0)), constant_values=-1)
            jt = jnp.concatenate([seq_p[:nw], seq_p[1:]], axis=1)
            it = seq[:, :, None]
            jb = jt[:, None, :]
            mask = (it < jb) | (it > jb + w) | (jb == -1)
            sim = jnp.einsum('bhwie,bhwje->bhwij', bq, bk2) * QK_SCALE
            sim = jnp.where(mask, -jnp.finfo(sim.dtype).max, sim)
            attn = jax.nn.softmax(sim, -1)
            out = jnp.einsum('bhwij,bhwje->bhwie', attn, bv2)
            return out.reshape(b, h, n, d)

        def attn_layer(x, Wqkv, qs, ksc, Wo):
            b, n, _ = x.shape
            qkv = x @ Wqkv
            q, k, v = jnp.split(qkv, 3, -1)
            sh = lambda t: t.reshape(b, n, HEADS, DIM_HEAD).transpose(0, 2, 1, 3)
            q, k, v = (sh(q), sh(k), sh(v))
            q = l2norm(q) * qs
            k = l2norm(k) * ksc
            freqs, scale = rotary_tables(n)
            cos, sin = (jnp.cos(freqs), jnp.sin(freqs))
            q = q * cos * scale + rotate_half(q) * sin * scale
            inv = 1.0 / scale
            k = k * cos * inv + rotate_half(k) * sin * inv
            out = local_attention(q, k, v)
            out = out.transpose(0, 2, 1, 3).reshape(b, n, INNER)
            return out @ Wo

        def ffn_layer(x, g, bln, W1, b1, W2, b2):
            mu = x.mean(-1, keepdims=True)
            var = ((x - mu) ** 2).mean(-1, keepdims=True)
            xn = (x - mu) / jnp.sqrt(var + 1e-05) * g + bln
            hg = xn @ W1 + b1
            a, gate = jnp.split(hg, 2, -1)
            return a * jax.nn.gelu(gate, approximate=False) @ W2 + b2
        for i in range(DEPTH):
            x = attn_layer(shift_tokens(x), Wqkv[i], q_scale[i], k_scale[i], Wo[i]) + x
            x = ffn_layer(shift_tokens(x), ln_g[i], ln_b[i], W1[i], b1[i], W2[i], b2[i]) + x
        return x

    def _L1_attn_ref(x, W_Q, W_K, W_V, W_O):
        import jax, jax.numpy as jnp
        import numpy as np
        NUM_HEADS = 16
        D_MODEL = 128
        D_K = D_MODEL // NUM_HEADS
        MAX_SEQ_LEN = 512
        ROPE_BASE = 10000.0
        BATCH = 2
        SEQ_LEN = 256

        def _rope_tables(seq_len, d_k, base=ROPE_BASE):
            theta = 1.0 / base ** (jnp.arange(0, d_k, 2, dtype=jnp.float32) / d_k)
            m = jnp.arange(seq_len, dtype=jnp.float32)
            m_theta = jnp.outer(m, theta)
            ang = jnp.concatenate([m_theta, m_theta], axis=-1)
            return (jnp.cos(ang), jnp.sin(ang))

        def _apply_rope(x, cos, sin):
            d2 = x.shape[-1] // 2
            x1, x2 = (x[..., :d2], x[..., d2:])
            x_flip = jnp.concatenate([-x2, x1], axis=-1)
            return x * cos + x_flip * sin
        B, S, _ = x.shape

        def proj(W):
            y = jnp.einsum('bsd,ed->bse', x, W)
            return y.reshape(B, S, NUM_HEADS, D_K).transpose(0, 2, 1, 3)
        Q, K, V = (proj(W_Q), proj(W_K), proj(W_V))
        cos, sin = _rope_tables(S, D_K)
        Q = _apply_rope(Q, cos, sin)
        K = _apply_rope(K, cos, sin)
        scores = jnp.einsum('bhsd,bhtd->bhst', Q, K) / jnp.sqrt(jnp.float32(D_K))
        causal = jnp.tril(jnp.ones((S, S), dtype=bool))
        scores = jnp.where(causal[None, None], scores, -jnp.inf)
        attn = jax.nn.softmax(scores, axis=-1)
        out = jnp.einsum('bhst,bhtd->bhsd', attn, V)
        out = out.transpose(0, 2, 1, 3).reshape(B, S, D_MODEL)
        return jnp.einsum('bsd,ed->bse', out, W_O)

    def _L1_ffn_ref(X, g1, g2, Wq, Wkc, Wvc, Wo, Wr, expert_bias, sW1, sW2, sW3, eW1, eW2, eW3):
        import jax, jax.numpy as jnp
        import numpy as np
        D_MODEL = 128
        NUM_HEADS = 4
        NUM_EXPERTS = 8
        TOP_K = 2
        D_FF = 128
        EPS = 1e-06

        def _rmsnorm(x, g):
            return x * jax.lax.rsqrt(jnp.mean(x * x, axis=-1, keepdims=True) + EPS) * g

        def _swiglu(x, w1, w2, w3):
            return jax.nn.silu(x @ w1.T) * (x @ w3.T) @ w2.T
        B, S, d = X.shape
        H = NUM_HEADS
        dk = d // H
        scale = 1.0 / jnp.sqrt(jnp.float32(dk))
        nx = _rmsnorm(X, g1)
        Q = (nx @ Wq.T).reshape(B, S, H, dk).transpose(0, 2, 1, 3)
        Kc = nx @ Wkc.T
        Vc = nx @ Wvc.T
        scores = jnp.einsum('bhsd,btd->bhst', Q, Kc) * scale
        attn = jax.nn.softmax(scores, axis=-1)
        out = jnp.einsum('bhst,btd->bhsd', attn, Vc)
        out = out.transpose(0, 2, 1, 3).reshape(B, S, d) @ Wo.T
        X = X + out
        nx = _rmsnorm(X, g2)
        xf = nx.reshape(-1, d)
        logits = xf @ Wr.T + expert_bias
        rw = jax.nn.softmax(logits, axis=-1)
        topw, topi = jax.lax.top_k(rw, TOP_K)
        topw = jax.nn.softmax(topw, axis=-1)
        combine = jnp.sum(jax.nn.one_hot(topi, NUM_EXPERTS, dtype=xf.dtype) * topw[..., None], axis=1)
        shared = _swiglu(xf, sW1, sW2, sW3)
        h = jax.nn.silu(jnp.einsum('td,efd->etf', xf, eW1)) * jnp.einsum('td,efd->etf', xf, eW3)
        eo = jnp.einsum('etf,edf->etd', h, eW2)
        specialist = jnp.einsum('te,etd->td', combine, eo)
        moe_out = (shared + specialist).reshape(B, S, d)
        return X + moe_out
    x = L0_attn_x
    x = x + _L0_attn_ref(_layernorm(x, axis=-1), L0_attn_wq, L0_attn_bq, L0_attn_wk, L0_attn_bk, L0_attn_wv, L0_attn_bv, L0_attn_wo, L0_attn_bo)
    x = x + _L0_ffn_ref(_layernorm(x, axis=-1), L0_ffn_Wqkv, L0_ffn_q_scale, L0_ffn_k_scale, L0_ffn_Wo, L0_ffn_ln_g, L0_ffn_ln_b, L0_ffn_W1, L0_ffn_b1, L0_ffn_W2, L0_ffn_b2)
    x = x + _L1_attn_ref(_layernorm(x, axis=-1), L1_attn_W_Q, L1_attn_W_K, L1_attn_W_V, L1_attn_W_O)
    x = x + _L1_ffn_ref(_layernorm(x, axis=-1), L1_ffn_g1, L1_ffn_g2, L1_ffn_Wq, L1_ffn_Wkc, L1_ffn_Wvc, L1_ffn_Wo, L1_ffn_Wr, L1_ffn_expert_bias, L1_ffn_sW1, L1_ffn_sW2, L1_ffn_sW3, L1_ffn_eW1, L1_ffn_eW2, L1_ffn_eW3)
    return x

_drawn_inputs = setup_inputs


def setup_inputs(seed=0):
    import zlib

    import numpy as np

    out = dict(_drawn_inputs(seed))
    spreads = {'L0_ffn_q_scale': (1.0, 0.6),
     'L0_ffn_k_scale': (1.0, 0.6),
     'L0_ffn_ln_g': (1.0, 0.6),
     'L0_ffn_ln_b': (0.0, 0.8),
     'L0_ffn_b1': (0.0, 0.8),
     'L0_ffn_b2': (0.0, 0.1),
     'L1_ffn_g1': (1.0, 0.6),
     'L1_ffn_g2': (1.0, 0.6),
     'L1_ffn_expert_bias': (0.0, 0.8)}
    factors = {'L0_attn_wq': 8.0,
     'L0_attn_bq': 8.0,
     'L0_attn_wk': 8.0,
     'L0_attn_bk': 8.0,
     'L0_attn_wv': 8.0,
     'L0_attn_bv': 8.0,
     'L0_attn_wo': 8.0,
     'L0_ffn_W1': 3.651,
     'L0_ffn_W2': 3.584,
     'L1_attn_W_Q': 8.0,
     'L1_attn_W_K': 8.0,
     'L1_ffn_Wq': 8.0,
     'L1_ffn_Wkc': 8.0,
     'L1_ffn_Wvc': 8.0,
     'L1_ffn_Wo': 8.0,
     'L1_ffn_Wr': 8.0,
     'L1_ffn_sW1': 8.0,
     'L1_ffn_sW2': 8.0,
     'L1_ffn_sW3': 8.0,
     'L1_ffn_eW1': 8.0,
     'L1_ffn_eW2': 8.0,
     'L1_ffn_eW3': 8.0}
    for name, (base, spread) in spreads.items():
        noise = np.random.default_rng([zlib.crc32(name.encode()), seed]).standard_normal(out[name].shape)
        drawn = base * np.exp(spread * noise) if base else spread * noise
        out[name] = jnp.asarray(drawn.astype(out[name].dtype))
    for name, factor in factors.items():
        out[name] = (out[name] * factor).astype(out[name].dtype)
    return out
```

```python
from contextlib import ExitStack

import numpy as np

import concourse.bass as bass
from concourse import mybir

F32 = mybir.dt.float32
F32R = mybir.dt.float32r
BF16 = mybir.dt.bfloat16
U32 = mybir.dt.uint32
ACT = mybir.ActivationFunctionType
ALU = mybir.AluOpType
AX = mybir.AxisListType

P = 128
D = 128
BATCH, SEQ = 4, 1024
TILES = SEQ // P
NT = BATCH * TILES
BANK = 512
CHUNKS = SEQ // BANK
TPB = BANK // P

HEADS_PER_UNIT = 4
ROWS = P // HEADS_PER_UNIT
MASKED = -1.0e30

DEPTH, LHEADS, LDIM, WINDOW = 6, 16, 64, 32
INNER = LHEADS * LDIM
FF = int(D * 4 * 2 / 3)
QK_SCALE = 8.0
WPT = P // WINDOW
HPC = BANK // LDIM
PAIRS = LHEADS // 2
ROUNDS, LAGS, BACK = 12, (0, 14, 23, 29), 3
TABLES = 2
FBLOCKS = [(k, min(P, FF - k)) for k in range(0, FF, P)]

DHEADS, DDIM = 4, 32
EXPERTS = 8
CONST_WIDTH = 3 * P + 4 * WINDOW + EXPERTS


class Engine:

    def __init__(self, queue, semaphore):
        self.queue, self.semaphore, self.count, self.passed = queue, semaphore, 0, {}

    def wait(self, *events):
        for event in events:
            if isinstance(event, list):
                self.wait(*event)
            elif event is not None and self.passed.get(event[0].name, 0) < event[1]:
                self.passed[event[0].name] = event[1]
                self.queue.wait_ge(event[0], event[1])

    def do(self, instruction, *events, signal=True):
        self.wait(*events)
        made = instruction(self.queue)
        if not signal:
            return None
        self.count += 1
        made.then_inc(self.semaphore, 1)
        return self.semaphore, self.count

    def dma(self, out, in_, channel, *events):
        self.wait(*events)
        channel.count += 16
        self.queue.dma_start(out, in_).then_inc(channel.semaphore, 16)
        return channel.semaphore, channel.count

    def last(self):
        return (self.semaphore, self.count) if self.count else None


class Channel:

    def __init__(self, semaphore):
        self.semaphore, self.count = semaphore, 0


class Ring:

    def __init__(self, views):
        self.views, self.free, self.at = views, [[] for _ in views], -1

    def take(self):
        self.at = (self.at + 1) % len(self.views)
        freed, self.free[self.at] = self.free[self.at], None
        assert freed is not None, "a buffer is taken before its last use is queued"
        return self.at, self.views[self.at], freed

    def release(self, slot, *events):
        self.free[slot] = list(events)


def weave(main, side, per=1):
    for _ in main:
        for _ in range(per):
            next(side, None)
    for _ in side:
        pass


def chain(*parts):
    for part in parts:
        yield from part


def bcast(ap, axis, n):
    shape = list(ap.shape)
    return ap.unsqueeze(axis).to_broadcast(shape[:axis] + [n] + shape[axis:])


def rotary_constants():
    f = np.float32
    t = np.arange(SEQ, dtype=f)
    theta = f(10000.0) ** (f(-2.0) * np.arange(4, dtype=f) / f(8))
    ang = t[:, None] * theta[None, :]
    cos_a, sin_a = np.repeat(np.cos(ang), 2, -1), np.repeat(np.sin(ang), 2, -1)
    theta = f(1.0) / f(10000.0) ** (np.arange(0, 8, 2, dtype=f) / f(8))
    ang = np.concatenate([t[:, None] * theta[None, :]] * 2, -1)
    cos_c, sin_c = np.cos(ang), np.sin(ang)
    sign = np.array([-1] * 4 + [1] * 4, f)
    small = np.concatenate([cos_a, sin_a * sign, cos_c, sin_c * sign], -1)
    half = np.arange(0, LDIM, 2, dtype=f)
    freqs = t[:, None] * (f(1.0) / f(10000.0) ** (half / f(LDIM)))[None, :]
    base = (half + f(0.4 * LDIM)) / f(1.4 * LDIM)
    power = (t - SEQ // 2) / f(WINDOW // 2)
    scale = base[None, :] ** power[:, None]
    cos, sin = np.cos(freqs), np.sin(freqs)
    local = np.concatenate([cos * scale * f(QK_SCALE), sin * scale * f(QK_SCALE),
                            cos / scale, sin / scale], -1)
    by_tile = lambda a: np.ascontiguousarray(
        a.astype(f).reshape(TILES, P, -1).transpose(1, 0, 2).reshape(P, -1))
    return by_tile(small), by_tile(local)


def mask_constants():
    i = np.arange(P)
    causal_qk = np.where(i[:, None] < i[None, :], MASKED, 0.0)
    q, k = np.arange(WINDOW)[:, None], np.arange(2 * WINDOW)[None, :] - WINDOW
    window = np.where((q < k) | (q > k + WINDOW), MASKED, 0.0)
    first = np.where(k < 0, MASKED, window)
    usual = np.tile(window, (WPT, 1))
    opening = np.concatenate([first] + [window] * (WPT - 1), 0)
    numbers = np.tile(np.arange(EXPERTS), (P, 1))
    return np.concatenate([np.eye(P), causal_qk, causal_qk.T, usual, opening, numbers], 1).astype(np.float32)


def build(nc, ins, out, stages="ABCD"):
    with ExitStack() as whole:
        enter = whole.enter_context
        pe = Engine(nc.tensor, enter(nc.semaphore("tensor_done")))
        act = Engine(nc.scalar, enter(nc.semaphore("scalar_done")))
        dve = Engine(nc.vector, enter(nc.semaphore("vector_done")))
        pool = Engine(nc.gpsimd, enter(nc.semaphore("gpsimd_done")))
        sp = Engine(nc.sync, enter(nc.semaphore("sync_done")))

        def channel(name):
            return Channel(enter(nc.semaphore(f"dma_{name}")))

        def sb(scope, name, shape, dt=F32):
            return scope.enter_context(nc.sbuf_tensor(name, [P] + list(shape), dt))

        def everyone_waits():
            events = [e.last() for e in (pe, act, dve, pool)]
            for e in (pe, act, dve, pool, sp):
                e.wait(*events)

        psum = enter(nc.psum_tensor("psum", [P, 8, BANK], F32))
        banks = [psum[:, n, :] for n in range(8)]

        x = sb(whole, "x", [NT, D])
        y = sb(whole, "y", [NT, D])
        ident = sb(whole, "ident", [P])
        ident_bf = sb(whole, "ident_bf", [P], BF16)
        ones = sb(whole, "ones", [P])
        moments = sb(whole, "moments", [2, TILES, 6])
        mean_var = sb(whole, "mean_var", [2, TILES, 2])
        spread = sb(whole, "spread", [2, TILES, 2])
        eps_ln = sb(whole, "eps_ln", [1])
        eps_rms = sb(whole, "eps_rms", [1])

        ch_x = [channel(f"x{b}") for b in range(BATCH)]
        ch_const = channel("constants")
        masks_f = y[:, :, :].rearrange("p t d -> p (t d)")[:, 0:2 * P + 4 * WINDOW]
        masks = sb(whole, "masks", [2 * P + 4 * WINDOW], BF16)
        causal_qk, causal_kq = masks[:, 0:P], masks[:, P:2 * P]
        window_mask, opening_mask = (masks[:, 2 * P + 2 * WINDOW * k:2 * P + 2 * WINDOW * (k + 1)]
                                     for k in range(2))
        small_rot = sb(whole, "small_rot", [TILES, 32])
        sp.dma(ident[:, :], ins["c_masks"][:, 0:P], ch_const)
        x_in = ins["L0_attn_x"].rearrange("b (t p) d -> b p t d", p=P)
        x_loaded = [sp.dma(x[:, TILES * b:TILES * (b + 1), :], x_in[b], ch_x[b]) for b in range(BATCH)]
        sp.dma(masks_f, ins["c_masks"][:, P:CONST_WIDTH - EXPERTS], ch_const)
        const_loaded = sp.dma(small_rot[:, :, :], ins["c_small"].rearrange("p (t c) -> p t c", t=TILES),
                              ch_const)
        pool.do(lambda e: e.memset(ones[:, :], 1.0))
        pool.do(lambda e: e.memset(eps_ln[:, :], 1e-5))
        ones_set = pool.do(lambda e: e.memset(eps_rms[:, :], 1e-6))
        dve.do(lambda e: e.tensor_copy(masks[:, :], masks_f), const_loaded)
        const_ready = dve.do(lambda e: e.tensor_copy(ident_bf[:, :], ident[:, :]))
        act.wait(ones_set)
        pe.wait(const_loaded, const_ready, ones_set)

        norm_slot = Ring([0, 1])

        def normalise(src, dst, ready, dst_free, rms=False):
            slot, _, freed = norm_slot.take()
            mo, mv, sd = moments[:, slot], mean_var[:, slot], spread[:, slot]
            for t in range(TILES):
                seen = dve.do(lambda e, t=t: e.bn_stats(mo[:, t, :], src[:, t, :]), ready, freed)
            for t in range(TILES):
                got = dve.do(lambda e, t=t: e.bn_aggr(mv[:, t, :], mo[:, t, :]), seen)
            if rms:
                got = dve.do(lambda e: e.tensor_tensor(sd[:, :, 0], mv[:, :, 0], mv[:, :, 0], ALU.mult), got)
                got = dve.do(lambda e: e.tensor_tensor(mv[:, :, 1], mv[:, :, 1], sd[:, :, 0], ALU.add), got)
            eps = eps_rms if rms else eps_ln
            root = act.do(lambda e: e.activation(sd[:, :, 0], mv[:, :, 1], ACT.Sqrt, bias=eps[:, 0:1]), got)
            inv = dve.do(lambda e: e.reciprocal(sd[:, :, 1], sd[:, :, 0]), root)
            for t in range(TILES):
                if rms:
                    end = dve.do(lambda e, t=t: e.tensor_scalar(
                        dst[:, t, :], src[:, t, :], sd[:, t, 1:2], None, ALU.mult), inv, dst_free)
                else:
                    end = dve.do(lambda e, t=t: e.tensor_scalar(
                        dst[:, t, :], src[:, t, :], mv[:, t, 0:1], sd[:, t, 1:2],
                        ALU.subtract, ALU.mult), inv, dst_free)
            norm_slot.release(slot, end)
            return end

        def transpose_tiles(src, dst, ring, ready, dst_free, evacuate=None, engine=act):
            done = []
            for c in range(CHUNKS):
                slot, bank, freed = ring.take()
                for t in range(TPB):
                    turned = pe.do(lambda e, t=t: e.transpose(
                        bank[:, P * t:P * (t + 1)], src[:, TPB * c + t, :], ident[:, :]),
                        ready, freed, signal=t == TPB - 1)
                move = evacuate or (lambda e, o, i: e.copy(o, i) if engine is act else e.tensor_copy(o, i))
                got = engine.do(lambda e: move(e, dst[:, BANK * c:BANK * (c + 1)], bank), turned, dst_free)
                ring.release(slot, got)
                done.append(got)
            return done

        def transposed_weight(scope, name, source, rows, ring, ch):
            raw = sb(scope, f"{name}_raw", [D])
            turned = sb(scope, name, [rows])
            loaded = sp.dma(raw[0:rows, :], source, ch)
            slot, bank, freed = ring.take()
            t = pe.do(lambda e: e.transpose(bank[:, 0:rows], raw[0:rows, :], ident[0:rows, 0:rows]), loaded, freed)
            got = dve.do(lambda e: e.tensor_copy(turned[:, :], bank[:, 0:rows]), t)
            ring.release(slot, got)
            return turned, got

        class FullAttention:

            def __init__(self, scope, name, dim, causal, scale, own_keys):
                self.dim, self.causal, self.scale, self.own_keys = dim, causal, scale, own_keys
                self.width = ROWS if own_keys else P
                self.nq = 1 if own_keys else HEADS_PER_UNIT
                self.units = 16 // HEADS_PER_UNIT if own_keys else 1
                heads = self.units * HEADS_PER_UNIT
                kheads = heads if own_keys else 1
                nk = HEADS_PER_UNIT if own_keys else 1
                w = self.width
                self.qx = Ring([sb(scope, f"{name}_qx{n}", [TILES, heads, w], F32R) for n in range(1)])
                self.kx = sb(scope, f"{name}_kx", [TILES, kheads, w], F32R)
                self.q1 = Ring([sb(scope, f"{name}_q1_{n}", [self.nq, SEQ], F32R) for n in range(1)])
                self.q2 = Ring([sb(scope, f"{name}_q2_{n}", [self.nq, SEQ], F32R) for n in range(2)])
                self.kt = Ring([sb(scope, f"{name}_kt{n}", [nk, SEQ], F32R) for n in range(2)])
                self.top2 = sb(scope, f"{name}_top2", [TILES, HEADS_PER_UNIT, CHUNKS])
                self.top = sb(scope, f"{name}_top", [TILES, HEADS_PER_UNIT])
                self.v = Ring([sb(scope, f"{name}_v{n}", [TILES, kheads, ROWS]) for n in range(2)])
                self.prob = Ring([sb(scope, f"{name}_prob{n}", [BANK]) for n in range(8)])
                self.ot = sb(scope, f"{name}_ot", [SEQ])
                self.ot_free = self.rsum_free = None
                self.o = sb(scope, f"{name}_o", [TILES, D])
                self.o_free = None
                if own_keys:
                    self.score_banks, self.side = Ring(banks[0:3]), Ring(banks[3:6])
                else:
                    self.score_banks, self.side, self.sum_banks = Ring(banks[0:2]), Ring(banks[2:4]), banks[4:6]
                self.out_banks = banks[6:8]
                self.out_free = None
                self.top_free = None
                zeroed = []
                for t in self.qx.views + [self.kx] + self.kt.views:
                    zeroed.append(pool.do(lambda e, t=t: e.memset(t[:].bitcast(F32), 0.0)))
                for t in self.v.views:
                    zeroed.append(pool.do(lambda e, t=t: e.memset(t[:], 0.0)))
                z = zeroed[-1]
                mid = 3 * dim
                z = pool.do(lambda e: e.memset(self.kx[:, :, :, mid:mid + 2].bitcast(F32), 1.0), z)
                if own_keys:
                    for t in self.v.views:
                        z = pool.do(lambda e, t=t: e.memset(t[:, :, :, dim:dim + 1], 1.0), z)
                self.cleared = z
                self.kx_free = None

            def split(self, engine, src, dst, order, ready, freed):
                d = self.dim
                high = order.index("h")
                first = engine.do(lambda e: e.tensor_copy(dst[:, :, :, high * d:(high + 1) * d], src), ready, freed)
                for n, part in enumerate(order):
                    if n == high:
                        continue
                    o = dst[:, :, :, n * d:(n + 1) * d]
                    h = dst[:, :, :, high * d:(high + 1) * d].bitcast(F32)
                    if part == "h":
                        end = engine.do(lambda e, o=o: e.tensor_copy(o, h), first)
                    else:
                        end = engine.do(lambda e, o=o: e.tensor_tensor(o, src, h, ALU.subtract), first)
                return end

            def turn(self, src, unit, dst, ready, dst_free, blocks):
                for n in range(blocks):
                    for c in range(CHUNKS):
                        slot, bank, freed = self.side.take()
                        for t in range(TPB):
                            lo = unit * HEADS_PER_UNIT if self.own_keys else n
                            hi = lo + (HEADS_PER_UNIT if self.own_keys else 1)
                            turned = pe.do(lambda e, t=t, lo=lo, hi=hi: e.transpose(
                                bank[:, P * t:P * (t + 1)],
                                src[:, TPB * c + t, lo:hi, :].rearrange("p h w -> p (h w)").bitcast(F32),
                                ident[:, :]), ready, freed, signal=t == TPB - 1)
                        yield n, c, slot, bank, turned

            def unit_first(self, b, unit, state):
                qx, kx = state["qx"], self.kx
                kslot, kt, kfreed = self.kt.take()
                for n, c, slot, bank, turned in self.turn(kx, unit, kt, state["k_split"], None, 1):
                    cols = slice(BANK * c, BANK * (c + 1))
                    if self.own_keys:
                        for g in range(HEADS_PER_UNIT):
                            rows = slice(ROWS * g, ROWS * (g + 1))
                            end = act.do(lambda e, g=g, rows=rows: e.copy(kt[rows, g, cols], bank[rows, :]),
                                         turned, kfreed, self.cleared)
                    else:
                        end = act.do(lambda e: e.copy(kt[:, 0, cols], bank), turned, kfreed, self.cleared)
                    self.side.release(slot, end)
                    yield
                k_ready = end
                self.kx_free = turned
                q1slot, q1, q1freed = self.q1.take()
                for n, c, slot, bank, turned in self.turn(qx, unit, q1, state["q_split"], None, self.nq):
                    end = act.do(lambda e: e.copy(q1[:, n, BANK * c:BANK * (c + 1)], bank), turned, q1freed)
                    self.side.release(slot, end)
                    yield
                q1_ready, turned_once = end, turned
                for t in range(TILES):
                    for g in range(HEADS_PER_UNIT):
                        lhs = q1[:, g if self.nq > 1 else 0, P * t:P * (t + 1)]
                        width = (t + 1) * P if self.causal else SEQ
                        for c in range(-(-width // BANK)):
                            hi = min(width, BANK * (c + 1))
                            n = hi - BANK * c
                            slot, bank, freed = self.side.take()
                            diagonal = self.causal and hi == width
                            rhs = kt[:, g if self.own_keys else 0, BANK * c:hi]
                            if diagonal:
                                pe.do(lambda e: e.matmul(
                                    bank[:, n - P:n], ident_bf[:, :], causal_qk, start=True, stop=False,
                                    skip_group_check=True), freed, signal=False)
                            got = pe.do(lambda e: e.matmul(
                                bank[:, 0:n], lhs, rhs, start=not diagonal, stop=True, skip_group_check=diagonal),
                                k_ready, q1_ready, freed)
                            end = dve.do(lambda e, n=n: e.tensor_reduce(
                                self.top2[:, t, g, c:c + 1], bank[:, 0:n], AX.X, ALU.max), got, self.top_free)
                            self.side.release(slot, end)
                            yield
                        if self.causal and c + 1 < CHUNKS:
                            end = dve.do(lambda e: e.tensor_copy(self.top2[:, t, g, 1:2], self.top2[:, t, g, 0:1]), end)
                self.q1.release(q1slot, got)
                top, heads = self.top, slice(unit * HEADS_PER_UNIT, (unit + 1) * HEADS_PER_UNIT)
                m = dve.do(lambda e: e.tensor_reduce(top[:, :, :], self.top2[:, :, :, :], AX.X, ALU.max, negate=True), end)
                mh = qx[:, :, heads, 3 * self.dim]
                ml = qx[:, :, heads, 3 * self.dim + 1]
                m = dve.do(lambda e: e.tensor_copy(mh, top[:, :, :]), m, turned_once)
                m = dve.do(lambda e: e.tensor_tensor(ml, top[:, :, :], mh.bitcast(F32), ALU.subtract), m)
                self.top_free = m
                q2slot, q2, q2freed = self.q2.take()
                for n, c, slot, bank, turned in self.turn(qx, unit, q2, m, None, self.nq):
                    end = act.do(lambda e: e.copy(q2[:, n, BANK * c:BANK * (c + 1)], bank), turned, q2freed)
                    self.side.release(slot, end)
                    yield
                if unit == self.units - 1:
                    self.qx.release(state["qslot"], turned)
                state[unit] = (kslot, kt, k_ready, q2slot, q2, end)

            def unit_second(self, b, unit, state):
                kslot, kt, k_ready, q2slot, q2, q_ready = state.pop(unit)
                v, v_ready = state["v"], state["v_ready"]
                started = set()
                waiting = []

                def values(group):
                    for g, c, lo, pslot, prob, ready, kt_i in group:
                        head = (unit * HEADS_PER_UNIT + g) if self.own_keys else 0
                        first = (g, c) not in started
                        started.add((g, c))
                        last = kt_i == (min(TILES, TPB * (c + 1)) - 1 if self.causal else TILES - 1)
                        o = self.out_banks[c][ROWS * g:ROWS * (g + 1), lo:BANK]
                        done = pe.do(lambda e, o=o, kt_i=kt_i, head=head, prob=prob, lo=lo, first=first, last=last: e.matmul(
                            o, v[:, kt_i, head, :], prob[:, lo:BANK], start=first, stop=last,
                            skip_group_check=True, tile_position=(0, ROWS * g)), ready, v_ready, self.out_free)
                        if not self.own_keys:
                            s = self.sum_banks[c][ROWS * g:ROWS * (g + 1), lo:BANK]
                            done = pe.do(lambda e, s=s, prob=prob, lo=lo, first=first, last=last: e.matmul(
                                s, ones[:, 0:ROWS], prob[:, lo:BANK], start=first, stop=last,
                                skip_group_check=True, tile_position=(0, ROWS * g)))
                        self.prob.release(pslot, done)
                    return done

                for kt_i in range(TILES):
                    for c in range(CHUNKS):
                        lo = max(0, kt_i * P - c * BANK) if self.causal else 0
                        if lo >= BANK:
                            continue
                        group = []
                        for g in range(HEADS_PER_UNIT):
                            slot, bank, freed = self.score_banks.take()
                            lhs = kt[:, g if self.own_keys else 0, P * kt_i:P * (kt_i + 1)]
                            rhs = q2[:, g if self.nq > 1 else 0, BANK * c + lo:BANK * (c + 1)]
                            diagonal = self.causal and kt_i * P >= c * BANK
                            if diagonal:
                                pe.do(lambda e: e.matmul(
                                    bank[:, lo:lo + P], ident_bf[:, :], causal_kq, start=True, stop=False,
                                    skip_group_check=True), freed, signal=False)
                            got = pe.do(lambda e: e.matmul(
                                bank[:, lo:BANK], lhs, rhs, start=not diagonal, stop=True, skip_group_check=diagonal),
                                k_ready, q_ready, freed)
                            pslot, prob, pfreed = self.prob.take()
                            ready = act.do(lambda e, bank=bank, prob=prob, lo=lo: e.activation(
                                prob[:, lo:BANK], bank[:, lo:BANK], ACT.Exp, scale=self.scale), got, pfreed)
                            self.score_banks.release(slot, ready)
                            group.append((g, c, lo, pslot, prob, ready, kt_i))
                            yield
                        waiting.append(group)
                        if len(waiting) > 1:
                            values(waiting.pop(0))
                        yield
                done = values(waiting.pop(0))
                self.kt.release(kslot, got)
                self.q2.release(q2slot, got)
                self.finish(unit, done)
                if unit == self.units - 1:
                    self.v.release(state["vslot"], done)
                yield

            def finish(self, unit, done):
                ot, o = self.ot, self.o
                for c in range(CHUNKS):
                    if self.own_keys:
                        end = dve.do(lambda e, c=c: e.tensor_copy(ot[:, BANK * c:BANK * (c + 1)], self.out_banks[c]),
                                     done, self.ot_free)
                    else:
                        r = dve.do(lambda e, c=c: e.reciprocal(ot[:, BANK * c:BANK * (c + 1)], self.sum_banks[c]),
                                   done, self.ot_free)
                        end = dve.do(lambda e, c=c: e.tensor_tensor(
                            ot[:, BANK * c:BANK * (c + 1)], self.out_banks[c], ot[:, BANK * c:BANK * (c + 1)],
                            ALU.mult), r)
                self.out_free = end
                if not self.own_keys:
                    self.ot_ready = end
                    return
                for c in range(CHUNKS):
                    slot, bank, freed = self.side.take()
                    for t in range(TPB):
                        turned = pe.do(lambda e, t=t, c=c: e.transpose(
                            bank[:, P * t:P * (t + 1)], ot[:, P * (TPB * c + t):P * (TPB * c + t + 1)],
                            ident[:, :]), end, freed, signal=t == TPB - 1)
                    heads = bank.rearrange("p (t g w) -> p t g w", t=TPB, g=HEADS_PER_UNIT)
                    r = dve.do(lambda e: e.reciprocal(self.rsum[:, :, :], heads[:, :, :, self.dim]), turned, self.rsum_free)
                    dst = o[:, TPB * c:TPB * (c + 1), unit * 32:(unit + 1) * 32].rearrange(
                        "p t (g d) -> p t g d", g=HEADS_PER_UNIT)
                    got = dve.do(lambda e: e.tensor_tensor(
                        dst, heads[:, :, :, 0:self.dim], bcast(self.rsum[:, :, :], 3, self.dim), ALU.mult),
                        r, self.o_free)
                    self.side.release(slot, got)
                    self.rsum_free = got
                self.ot_free = turned
                self.o_ready = got

        def pipeline(att, prepare, conclude):
            states = [dict() for _ in range(BATCH)]
            order = [(b, u) for b in range(BATCH) for u in range(att.units)]

            def first(i):
                if i >= len(order):
                    return
                b, u = order[i]
                if u == 0:
                    yield from prepare(b, states[b])
                yield from att.unit_first(b, u, states[b])

            for _ in first(0):
                pass
            ending = iter(())
            for i, (b, u) in enumerate(order):
                weave(att.unit_second(b, u, states[b]), chain(ending, first(i + 1)))
                ending = conclude(b, states[b]) if u == att.units - 1 else iter(())
            for _ in ending:
                pass

        def mha_stage(name, w_names, biases, rot, causal):
            with ExitStack() as scope:
                att = FullAttention(scope, name, 8, causal, float(1.0 / np.sqrt(np.float32(8))), True)
                side = att.side
                att.rsum = sb(scope, f"{name}_rsum", [TPB, HEADS_PER_UNIT])
                ch = channel(f"{name}_w")
                w_qkv = sb(scope, f"{name}_w_qkv", [3 * D])
                w_out = sb(scope, f"{name}_w_out", [D])
                raw = sb(scope, f"{name}_raw", [4, D])
                for n, w in enumerate(w_names):
                    loaded = sp.dma(raw[:, n, :], ins[w], ch)
                slot, bank, freed = side.take()
                for n in range(4):
                    t = pe.do(lambda e, n=n: e.transpose(bank[:, D * n:D * (n + 1)], raw[:, n, :], ident[:, :]),
                              loaded, freed)
                w_ready = dve.do(lambda e: e.tensor_copy(w_qkv[:, :], bank[:, 0:3 * D]), t)
                w_ready = dve.do(lambda e: e.tensor_copy(w_out[:, :], bank[:, 3 * D:4 * D]), t)
                side.release(slot, w_ready)
                if biases:
                    ch_bias = channel(f"{name}_bias")
                    bias = sb(scope, f"{name}_bias", [4 * D])
                    for n, v in enumerate(biases):
                        b_loaded = sp.dma(bias[:, D * n:D * (n + 1)], ins[v].partition_broadcast(P), ch_bias)
                xn = sb(scope, f"{name}_xn", [TILES, D])
                xnt = sb(scope, f"{name}_xnt", [SEQ])
                qkv = sb(scope, f"{name}_qkv", [TILES, 3 * D])
                turn1 = sb(scope, f"{name}_turn1", [TILES, 2 * D])
                turn2 = y[:, 0:2 * TILES, :].rearrange("p (t s) d -> p t (s d)", t=TILES)
                free = {"xn": None, "xnt": None, "qkv": None, "turn": None}

                def prepare(b, state):
                    xb = x[:, TILES * b:TILES * (b + 1), :]
                    normed = normalise(xb, xn, x_loaded[b], free["xn"])
                    yield
                    parts = transpose_tiles(xn, xnt, side, normed, free["xnt"])
                    free["xn"] = parts[-1]
                    yield
                    for t in range(TILES):
                        slot, bank, freed = side.take()
                        got = pe.do(lambda e: e.matmul(bank[:, 0:3 * D], xnt[:, P * t:P * (t + 1)], w_qkv[:, :],
                                                       start=True, stop=True), parts, w_ready, freed)
                        if biases:
                            end = dve.do(lambda e: e.tensor_tensor(qkv[:, t, :], bank[:, 0:3 * D], bias[:, 0:3 * D],
                                                                   ALU.add), got, b_loaded, free["qkv"])
                        else:
                            end = dve.do(lambda e: e.tensor_copy(qkv[:, t, :], bank[:, 0:3 * D]), got, free["qkv"])
                        side.release(slot, end)
                        yield
                    free["xnt"] = got
                    heads = lambda a, lo, hi: a[:, :, lo:hi].rearrange("p t (h d) -> p t h d", d=8)
                    for part in range(2):
                        q = heads(qkv, D * part, D * (part + 1))
                        t1 = heads(turn1, D * part, D * (part + 1))
                        t2 = heads(turn2, D * part, D * (part + 1))
                        cos = lambda lo, hi: bcast(small_rot[:, :, rot + lo:rot + hi], 2, 16)
                        a = dve.do(lambda e: e.tensor_tensor(t1, q, cos(0, 8), ALU.mult), end, free["turn"])
                        a = dve.do(lambda e: e.tensor_tensor(t2[:, :, :, 0:4], q[:, :, :, 4:8], cos(8, 12), ALU.mult), end)
                        a = dve.do(lambda e: e.tensor_tensor(t2[:, :, :, 4:8], q[:, :, :, 0:4], cos(12, 16), ALU.mult), end)
                        yield
                    rotated = dve.do(lambda e: e.tensor_tensor(turn1[:], turn1[:], turn2[:], ALU.add), a)
                    yield
                    qslot, qx, qfreed = att.qx.take()
                    state["qx"], state["qslot"] = qx, qslot
                    z = pool.do(lambda e: e.memset(qx[:, :, :, 24:26].bitcast(F32), 0.0), qfreed, att.cleared)
                    state["q_split"] = [z, att.split(dve, heads(turn1, 0, D), qx, "hhl", rotated, [att.cleared, qfreed])]
                    yield
                    state["k_split"] = att.split(dve, heads(turn1, D, 2 * D), att.kx, "hlh", rotated,
                                                 [att.cleared, att.kx_free])
                    free["turn"] = state["k_split"]
                    vslot, v, vfreed = att.v.take()
                    state["v"], state["vslot"] = v, vslot
                    state["v_ready"] = dve.do(lambda e: e.tensor_copy(v[:, :, :, 0:8], heads(qkv, 2 * D, 3 * D)),
                                              end, vfreed, att.cleared)
                    free["qkv"] = state["v_ready"]
                    if biases:
                        state["x"] = pool.do(lambda e: e.tensor_tensor(
                            xb, xb, bcast(bias[:, 3 * D:4 * D], 1, TILES), ALU.add), normed, b_loaded)
                    else:
                        state["x"] = normed
                    yield

                def conclude(b, state):
                    parts = transpose_tiles(att.o, xnt2, side, att.o_ready, free.get("xnt2"))
                    att.o_free = parts[-1]
                    yield
                    for c in range(CHUNKS):
                        slot, bank, freed = side.take()
                        for t in range(TPB):
                            got = pe.do(lambda e, t=t: e.matmul(
                                bank[:, P * t:P * (t + 1)], xnt2[:, P * (TPB * c + t):P * (TPB * c + t + 1)],
                                w_out[:, :], start=True, stop=True), parts, freed)
                        rows = x[:, TILES * b + TPB * c:TILES * b + TPB * (c + 1), :]
                        end = dve.do(lambda e: e.tensor_tensor(
                            rows, rows, bank.rearrange("p (t d) -> p t d", t=TPB), ALU.add), got, state["x"])
                        side.release(slot, end)
                        yield
                    free["xnt2"] = got

                xnt2 = sb(scope, f"{name}_xnt2", [SEQ])
                pipeline(att, prepare, conclude)
                everyone_waits()

        def local_stage():
            kept = nc.dram_tensor("kept_x", (P, NT, D), F32, kind="Internal").ap()
            with ExitStack() as scope:
                def buf(name, shape, dt=F32):
                    return sb(scope, f"b_{name}", shape, dt)

                proj, turns = Ring(banks[0:2]), Ring(banks[2:4])
                score, out_ring, ff_ring = Ring(banks[4:6]), Ring(banks[6:7]), Ring(banks[7:8])

                ch_small = channel("b_small")
                gain, shift_ = buf("gain", [DEPTH]), buf("shift", [DEPTH])
                b1 = buf("b1", [2, len(FBLOCKS), DEPTH])
                b2 = buf("b2", [DEPTH, D])
                qk_scale = buf("qk_scale", [2, DEPTH, LDIM])
                base_table = buf("base_table", [TILES, 4, LDIM // 2])
                with nc.allow_non_contiguous_dma(reason="parameters by feature, a few thousand words"):
                    sp.dma(gain[:, :], ins["L0_ffn_ln_g"].rearrange("l d -> d l"), ch_small)
                    sp.dma(shift_[:, :], ins["L0_ffn_ln_b"].rearrange("l d -> d l"), ch_small)
                    for part in range(2):
                        for n, (lo, size) in enumerate(FBLOCKS):
                            sp.dma(b1[0:size, part, n, :],
                                   ins["L0_ffn_b1"][:, FF * part + lo:FF * part + lo + size].rearrange("l f -> f l"),
                                   ch_small)
                for n, name in enumerate(("L0_ffn_q_scale", "L0_ffn_k_scale")):
                    sp.dma(qk_scale[:, n, :, :].rearrange("p l d -> p (l d)"),
                           ins[name].rearrange("l d -> (l d)").partition_broadcast(P), ch_small)
                sp.dma(b2[:, :, :].rearrange("p l d -> p (l d)"),
                       ins["L0_ffn_b2"].rearrange("l d -> (l d)").partition_broadcast(P), ch_small)
                small = sp.dma(base_table[:, :, :, :], ins["c_local"].rearrange(
                    "p (t k d) -> p t k d", t=TILES, k=4), ch_small)
                act.wait(small)
                pool.wait(small)

                w_qk = [buf(f"w_qk{n}", [2 * INNER]) for n in range(2)]
                w1, w2 = buf("w1", [2 * FF]), buf("w2", [len(FBLOCKS), D])
                w_v, w_o = buf("w_v", [INNER]), buf("w_o", [PAIRS, D])
                w_vt = w_v[:, :].rearrange("p (a b) -> p a b", a=PAIRS)
                w_vo = [buf(f"w_vo{n}", [4, 4, D]) for n in range(2)]
                table = [buf(f"table{n}", [TILES, 4, LDIM]) for n in range(TABLES)]
                ch_qk, ch_ff = [channel(f"b_qk{n}") for n in range(2)], channel("b_ff")
                ch_vo = channel("b_vo")
                layer = [dict() for _ in range(DEPTH)]
                use = {"qk": [None, None], "ff": None, "vo": [None, None], "raw": None,
                       "table": [None] * TABLES}

                def load_layer(l):
                    n, s = l % 2, layer[l]
                    s["qk"] = sp.dma(w_qk[n][:, :], ins["L0_ffn_Wqkv"][l, :, 0:2 * INNER], ch_qk[n], use["qk"][n])
                    sp.dma(w_v[:, :], ins["L0_ffn_Wqkv"][l, :, 2 * INNER:], ch_vo, use["raw"])
                    s["vo_raw"] = sp.dma(w_o[:, :, :], ins["L0_ffn_Wo"][l].rearrange("(c p) d -> p c d", p=P), ch_vo)

                def load_feed_forward(l):
                    full = FF // P
                    sp.dma(w1[:, :], ins["L0_ffn_W1"][l], ch_ff, use["ff"])
                    sp.dma(w2[:, 0:full, :], ins["L0_ffn_W2"][l, 0:full * P, :].rearrange(
                        "(c p) d -> p c d", p=P), ch_ff)
                    layer[l]["ff"] = sp.dma(w2[0:FF - full * P, full, :], ins["L0_ffn_W2"][l, full * P:, :], ch_ff)

                def prepare_layer(l):
                    n, tn, s = l % 2, l % TABLES, layer[l]
                    for k in range(4):
                        for half in (slice(0, LDIM // 2), slice(LDIM // 2, LDIM)):
                            s["table"] = pool.do(lambda e: e.tensor_tensor(
                                table[tn][:, :, k, half], base_table[:, :, k, :],
                                bcast(qk_scale[:, k // 2, l, half], 1, TILES), ALU.mult), use["table"][tn])
                        yield
                    for c in range(PAIRS // 4):
                        slot, bank, freed = turns.take()
                        for p in range(4):
                            lo = (4 * c + p) * P
                            t = pe.do(lambda e: e.transpose(bank[:, P * p:P * (p + 1)], w_v[:, lo:lo + P], ident[:, :]),
                                      s["vo_raw"], freed, signal=p == 3)
                        turned = dve.do(lambda e: e.tensor_copy(
                            w_vt[:, 4 * c:4 * (c + 1), :].rearrange("p a b -> p (a b)"), bank), t)
                        turns.release(slot, turned)
                        yield
                    for odd in range(2):
                        rows = slice(LDIM * odd, LDIM * (odd + 1))
                        for c in range(PAIRS // 4):
                            slot, bank, freed = turns.take()
                            for p in range(4):
                                t = pe.do(lambda e: e.matmul(
                                    bank[:, D * p:D * (p + 1)], w_vt[rows, 4 * c + p, :], w_o[rows, 4 * c + p, :],
                                    start=True, stop=True), turned, freed, signal=p == 3)
                            got = dve.do(lambda e: e.tensor_copy(
                                w_vo[n][:, odd::2, 2 * c:2 * (c + 1), :].rearrange("p g m d -> p m g d"),
                                bank.rearrange("p (m g d) -> p m g d", m=2, g=2)), t, use["vo"][n])
                            turns.release(slot, got)
                            yield
                    use["raw"], s["vo"] = t, got

                flat = x[:, :, :].rearrange("p t d -> p (t d)")
                part = [flat[:, BANK * n:BANK * (n + 1)] for n in range(8)]
                rot = Ring(part[0:6])
                square = Ring(part[6:8])
                cross = Ring([buf(f"cross{n}", [BANK]) for n in range(2)])
                norm = Ring([buf(f"norm{n}", [3, 2 * LHEADS]) for n in range(2)])
                xs = Ring([buf(f"xs{n}", [TILES, D]) for n in range(2)])
                xst = Ring([buf(f"xst{n}", [SEQ]) for n in range(2)])
                xnt = Ring([buf("xnt", [SEQ])])
                q_t = Ring([buf(f"q_t{n}", [PAIRS, P]) for n in range(2)])
                k_t = buf("k_t", [PAIRS, 2, 3, P])
                v_w = buf("v_w", [3 * WPT, 4, D])
                k_ring, v_ring = Ring([0, 1, 2]), Ring([0, 1, 2])
                prob = Ring([buf(f"prob{n}", [2, HPC, WINDOW]) for n in range(3)])
                prob_t = Ring([buf(f"prob_t{n}", [4, P]) for n in range(3)])
                stat = Ring([buf(f"stat{n}", [3, HPC]) for n in range(3)])
                gate = Ring([buf(f"gate{n}", [BANK]) for n in range(1)])
                hidden = Ring([buf(f"hidden{n}", [len(FBLOCKS), BANK]) for n in range(1)])
                ch_xs = [channel(f"b_xs{n}") for n in range(2)]
                z = [pool.do(lambda e: e.memset(k_t[:, :, :, :, :], 0.0))]
                act.wait(z[0])
                dve.wait(z[0])

                ch_kept = channel("b_kept")
                y_ready = []
                for b in range(BATCH):
                    tiles = slice(TILES * b, TILES * (b + 1))
                    y_ready.append([normalise(x[:, tiles, :], y[:, tiles, :], x_loaded[b], None)])
                x_kept = sp.dma(kept, x[:, :, :], ch_kept, x_loaded)
                for e in (dve, act, pool, pe):
                    e.wait(x_kept, y_ready[-1])

                def shifted(b):
                    slot, buffer, freed = xs.take()
                    t0, half, ch = TILES * b, D // 2, ch_xs[slot]
                    rows = y[:, t0:t0 + TILES, :]
                    z = pool.do(lambda e: e.memset(buffer[0:1, 0, half:D], 0.0), freed)
                    sp.dma(buffer[:, :, 0:half], rows[:, :, 0:half], ch, y_ready[b], freed, z)
                    sp.dma(buffer[1:P, :, half:D], rows[0:P - 1, :, half:D], ch)
                    moved = sp.dma(buffer[0:1, 1:TILES, half:D], rows[P - 1:P, 0:TILES - 1, half:D], ch)
                    return slot, buffer, [moved, z]

                batches, fed_forward = {}, set()

                def open_batch(l, b):
                    assert l == 0 or (l - 1, b) in fed_forward
                    slot, buffer, loaded = shifted(b)
                    yield
                    yield
                    tslot, turned, freed = xst.take()
                    ready = transpose_tiles(buffer, turned, turns, loaded, freed, engine=dve)
                    xs.release(slot, ready)
                    batches[l, b] = {"xst": turned, "slot": tslot, "ready": ready}
                    yield

                tiles = {}

                def project(l, b, t):
                    s, info = batches[l, b], {"rot": []}
                    tiles[l, b, t] = info
                    nslot, nm, nfreed = norm.take()
                    tab = table[l % TABLES]
                    for c in range(4):
                        slot, bank, freed = proj.take()
                        got = pe.do(lambda e: e.matmul(bank, s["xst"][:, P * t:P * (t + 1)],
                                                       w_qk[l % 2][:, BANK * c:BANK * (c + 1)], start=True, stop=True),
                                    s["ready"], layer[l]["qk"], freed)
                        heads = bank.rearrange("p (h d) -> p h d", h=HPC)
                        sslot, sq, sfreed = square.take()
                        squared = act.do(lambda e: e.activation(sq, bank, ACT.Square), got, sfreed)
                        yield
                        rslot, r, rfreed = rot.take()
                        cslot, x2, cfreed = cross.take()
                        k = 2 * (c // 2)
                        rh, xh = (a.rearrange("p (h d) -> p h d", h=HPC) for a in (r, x2[:, :]))
                        straight = dve.do(lambda e: e.tensor_tensor(
                            rh, heads, bcast(tab[:, t, k, :], 1, HPC), ALU.mult), squared, rfreed, layer[l]["table"])
                        crossed = dve.do(lambda e: e.tensor_tensor(
                            xh, heads, bcast(tab[:, t, k + 1, :], 1, HPC), ALU.mult), cfreed)
                        proj.release(slot, crossed)
                        summed = dve.do(lambda e: e.tensor_reduce(
                            nm[:, 0, HPC * c:HPC * (c + 1)], sq.rearrange("p (h d) -> p h d", h=HPC), AX.X, ALU.add),
                            squared, nfreed)
                        square.release(sslot, summed)
                        half = LDIM // 2
                        for a, o, op in ((0, half, ALU.subtract), (half, 0, ALU.add)):
                            added = pool.do(lambda e: e.tensor_tensor(
                                rh[:, :, a:a + half], rh[:, :, a:a + half], xh[:, :, o:o + half], op), crossed)
                        cross.release(cslot, added)
                        info["rot"].append((rslot, r, added))
                        yield
                    use["qk"][l % 2] = got
                    use["table"][l % TABLES] = crossed
                    root = act.do(lambda e: e.activation(nm[:, 1, :], nm[:, 0, :], ACT.Sqrt), summed)
                    held = dve.do(lambda e: e.tensor_scalar(nm[:, 2, :], nm[:, 1, :], 1e-12, None, ALU.max), root)
                    inv = dve.do(lambda e: e.reciprocal(nm[:, 0, :], nm[:, 2, :]), held)
                    for c, (rslot, r, added) in enumerate(info["rot"]):
                        rh = r.rearrange("p (h d) -> p h d", h=HPC)
                        scaled = pool.do(lambda e: e.tensor_tensor(
                            rh, rh, bcast(nm[:, 0, HPC * c:HPC * (c + 1)], 2, LDIM), ALU.mult), inv, added)
                        info["rot"][c] = (rslot, r, scaled)
                        yield
                    norm.release(nslot, scaled)

                def turn(l, b, t):
                    s, info = batches[l, b], tiles[l, b, t]
                    qslot, qt, qfreed = q_t.take()
                    kslot, _, kfreed = k_ring.take()
                    vslot, _, vfreed = v_ring.take()
                    for c in range(4):
                        rslot, r, scaled = info["rot"][c]
                        slot, bank, freed = turns.take()
                        for p in range(4):
                            turned = pe.do(lambda e: e.transpose(bank[:, P * p:P * (p + 1)], r[:, P * p:P * (p + 1)],
                                                                 ident[:, :]), scaled, freed, signal=p == 3)
                        rot.release(rslot, turned)
                        pairs = slice(4 * (c % 2), 4 * (c % 2) + 4)
                        by_pair = bank.rearrange("p (a q) -> p a q", a=4)
                        if c < 2:
                            got = act.do(lambda e: e.copy(qt[:, pairs, :], by_pair), turned, qfreed)
                            turns.release(slot, got)
                            info["q"] = got
                        else:
                            lo = act.do(lambda e: e.copy(k_t[0:LDIM, pairs, 0, kslot, :], by_pair[0:LDIM]),
                                        turned, kfreed)
                            hi = dve.do(lambda e: e.tensor_copy(k_t[LDIM:P, pairs, 1, kslot, :], by_pair[LDIM:P]),
                                        turned, kfreed)
                            turns.release(slot, lo, hi)
                            info["k"] = [lo, hi]
                        yield
                        w = c
                        slot, bank, freed = proj.take()
                        for g in range(4):
                            got = pe.do(lambda e: e.matmul(
                                bank[WINDOW * g:WINDOW * (g + 1), :],
                                s["xst"][:, P * t + WINDOW * w:P * t + WINDOW * (w + 1)],
                                w_vo[l % 2][:, g, :, :].rearrange("p m d -> p (m d)"), start=True, stop=True,
                                tile_position=(0, WINDOW * g)), layer[l]["vo"], freed, signal=g == 3)
                        v = v_w[:, WPT * vslot + w, :, :].rearrange("p m d -> p (m d)")
                        info["v"] = act.do(lambda e: e.copy(v, bank), got, vfreed)
                        proj.release(slot, info["v"])
                        yield
                    use["vo"][l % 2] = got
                    info.update(qslot=qslot, qt=qt, kslot=kslot, vslot=vslot)
                    if t == TILES - 1:
                        xst.release(s["slot"], got)

                def per_head(ap):
                    return bcast(bcast(ap, 1, 2), 3, WINDOW)

                def attend(l, b, t):
                    info = tiles[l, b, t]
                    before = tiles[l, b, t - 1] if t else None
                    mask = opening_mask if t == 0 else window_mask
                    ks, qt = info["kslot"], info["qt"]
                    info["prob"] = []
                    for c in range(2):
                        slot, bank, freed = score.take()
                        halves = bank.rearrange("p (s h k) -> p s h k", s=2, h=HPC)
                        pe.do(lambda e: e.matmul(
                            halves, ident_bf[:, :], bcast(mask.rearrange("p (s k) -> p s k", s=2), 2, HPC),
                            start=True, stop=False, skip_group_check=True),
                              freed, info["q"], info["k"], before and before["k"], signal=False)
                        by_head = bank.rearrange("p (s h k) -> p h s k", s=2, h=HPC)
                        for p in range(4):
                            for w in range(WPT):
                                q = qt[:, 4 * c + p, WINDOW * w:WINDOW * (w + 1)]
                                rows = slice(WINDOW * w, WINDOW * (w + 1))
                                k = k_t[:, 4 * c + p, :, :, :].rearrange("p h s q -> p h (s q)")
                                at = P * ks + WINDOW * (w - 1)
                                if w or (t and ks):
                                    spans = [(at, slice(0, 2))]
                                else:
                                    spans = [(at + WINDOW, slice(1, 2))]
                                    if t:
                                        spans.append((P * 3 - WINDOW, slice(0, 1)))
                                for lo, to in spans:
                                    n = WINDOW * (to.stop - to.start)
                                    got = pe.do(lambda e: e.matmul(
                                        by_head[rows, 2 * p:2 * p + 2, to, :], q, k[:, :, lo:lo + n].rearrange(
                                            "p h (s q) -> p h s q", q=WINDOW),
                                        start=False, stop=True, skip_group_check=True,
                                        tile_position=(0, WINDOW * w)), signal=p == 3 and w == WPT - 1)
                            if p == 1:
                                yield
                        sslot, st, sfreed = stat.take()
                        pslot, pr, pfreed = prob.take()
                        top = dve.do(lambda e: e.tensor_reduce(st[:, 0, :], by_head, AX.XY, ALU.max), got, sfreed)
                        less = dve.do(lambda e: e.tensor_tensor(
                            pr[:, :, :, :], halves, per_head(st[:, 0, :]), ALU.subtract), top, pfreed)
                        score.release(slot, less)
                        power = act.do(lambda e: e.activation(pr[:, :, :, :], pr[:, :, :, :], ACT.Exp), less)
                        yield
                        total = dve.do(lambda e: e.tensor_reduce(
                            st[:, 1, :], pr[:, :, :, :].rearrange("p s h k -> p h s k"), AX.XY, ALU.add), power)
                        inv = dve.do(lambda e: e.reciprocal(st[:, 2, :], st[:, 1, :]), total)
                        done = pool.do(lambda e: e.tensor_tensor(
                            pr[:, :, :, :], pr[:, :, :, :], per_head(st[:, 2, :]), ALU.mult), inv)
                        stat.release(sslot, done)
                        info["prob"].append((pslot, pr, done))
                        yield
                    q_t.release(info["qslot"], got)
                    if before:
                        k_ring.release(before["kslot"], got)
                    if t == TILES - 1:
                        k_ring.release(ks, got)

                def combine(l, b, t):
                    info = tiles[l, b, t]
                    before = tiles[l, b, t - 1] if t else None
                    oslot, obank, ofreed = out_ring.take()
                    started = set()
                    for c in range(2):
                        pslot, pr, ready = info["prob"][c]
                        slot, bank, freed = turns.take()
                        for j in range(4):
                            m, half = j // 2, j % 2
                            turned = pe.do(lambda e: e.transpose(
                                bank[:, P * j:P * (j + 1)],
                                pr[:, half, 4 * m:4 * (m + 1), :].rearrange("p g k -> p (g k)"), ident[:, :]),
                                ready, freed, signal=j == 3)
                        prob.release(pslot, turned)
                        tslot, pt, tfreed = prob_t.take()
                        got = act.do(lambda e: e.copy(pt[:, :, :].rearrange("p j q -> p (j q)"), bank), turned, tfreed)
                        turns.release(slot, got)
                        yield
                        for j in range(4):
                            m, half = 2 * c + j // 2, j % 2
                            for w in range(WPT):
                                if half == 0 and w == 0:
                                    if not t:
                                        continue
                                    at = WPT * before["vslot"] + WPT - 1
                                else:
                                    at = WPT * info["vslot"] + w - 1 + half
                                rows = slice(WINDOW * w, WINDOW * (w + 1))
                                done = pe.do(lambda e: e.matmul(
                                    obank[rows, 0:D], pt[:, j, rows], v_w[:, at, m, :], start=w not in started,
                                    stop=c == 1 and j == 3, skip_group_check=True, tile_position=(0, WINDOW * w)),
                                    got, info["v"], before and before["v"], ofreed, signal=j == 3 and w == WPT - 1)
                                started.add(w)
                        prob_t.release(tslot, done)
                        yield
                    rows = y[:, TILES * b + t, :]
                    end = dve.do(lambda e: e.tensor_tensor(rows, rows, obank[:, 0:D], ALU.add), done, y_ready[b])
                    out_ring.release(oslot, end)
                    info["y"] = end
                    if before:
                        v_ring.release(before["vslot"], done)
                    if t == TILES - 1:
                        v_ring.release(info["vslot"], done)
                        y_ready[b] = [end]

                def feed_forward(l, b):
                    s = layer[l]
                    slot, buffer, loaded = shifted(b)
                    yield
                    rows = y[:, TILES * b:TILES * (b + 1), :]
                    biased = pool.do(lambda e: e.tensor_tensor(rows, rows, bcast(b2[:, l, :], 1, TILES), ALU.add),
                                     loaded, y_ready[b])
                    yield
                    yield
                    normed = normalise(buffer, buffer, loaded, None)
                    yield
                    xslot, xn, xfreed = xnt.take()
                    ready = transpose_tiles(buffer, xn, ff_ring, normed, xfreed, evacuate=lambda e, o, i: e.activation(
                        o, i, ACT.Identity, bias=shift_[:, l:l + 1], scale=gain[:, l:l + 1]))
                    xs.release(slot, ready)
                    yield
                    for c in range(CHUNKS):
                        hslot, hid, hfreed = hidden.take()
                        for f, (lo, size) in enumerate(FBLOCKS):
                            for part in (1, 0):
                                bslot, bank, freed = ff_ring.take()
                                got = pe.do(lambda e: e.matmul(
                                    bank[0:size, :], w1[:, FF * part + lo:FF * part + lo + size],
                                    xn[:, BANK * c:BANK * (c + 1)], start=True, stop=True), ready, s["ff"], freed)
                                bias = b1[0:size, part, f, l:l + 1]
                                if part:
                                    gslot, gt, gfreed = gate.take()
                                    opened = act.do(lambda e: e.activation(gt[0:size, :], bank[0:size, :], ACT.Gelu,
                                                                           bias=bias), got, gfreed)
                                    ff_ring.release(bslot, opened)
                                else:
                                    made = dve.do(lambda e: e.scalar_tensor_tensor(
                                        out=hid[0:size, f, :], in0=bank[0:size, :], scalar=bias, in1=gt[0:size, :],
                                        op0=ALU.add, op1=ALU.mult), got, opened, hfreed)
                                    ff_ring.release(bslot, made)
                                    gate.release(gslot, made)
                                yield
                        bslot, bank, freed = ff_ring.take()
                        for t in range(TPB):
                            for f, (lo, size) in enumerate(FBLOCKS):
                                got = pe.do(lambda e: e.matmul(
                                    bank[:, P * t:P * (t + 1)], hid[0:size, f, P * t:P * (t + 1)], w2[0:size, f, :],
                                    start=f == 0, stop=f == len(FBLOCKS) - 1), made, freed,
                                    signal=t == TPB - 1 and f == len(FBLOCKS) - 1)
                            yield
                        hidden.release(hslot, got)
                        part = rows[:, TPB * c:TPB * (c + 1), :]
                        end = dve.do(lambda e: e.tensor_tensor(
                            part, part, bank.rearrange("p (t d) -> p t d", t=TPB), ALU.add), got, biased)
                        ff_ring.release(bslot, end)
                        yield
                    xnt.release(xslot, got)
                    use["ff"] = got
                    y_ready[b] = [end]
                    fed_forward.add((l, b))

                stream = [(l, b, t) for l in range(DEPTH) for b in range(BATCH) for t in range(TILES)]
                load_layer(0)
                for _ in prepare_layer(0):
                    pass
                for _ in open_batch(0, 0):
                    pass
                opening, preparing, fed, active = [], [], [], []
                last_start = ROUNDS * (len(stream) - 1) + max(LAGS)
                now = 0
                while now <= last_start or active:
                    for lag, stage in zip(LAGS, (project, turn, attend, combine)):
                        i, rest = divmod(now - lag, ROUNDS)
                        if rest or not 0 <= i < len(stream):
                            continue
                        l, b, t = stream[i]
                        active.append((i, stage(l, b, t)))
                        if stage is project:
                            if b == 0 and t == 3 and l + 1 < DEPTH:
                                load_layer(l + 1)
                            if b == 1 and t == 2:
                                load_feed_forward(l)
                            if b == 1 and t == 3 and l + 1 < DEPTH:
                                preparing.append(prepare_layer(l + 1))
                            if t == TILES - 2 and i + 2 < len(stream):
                                opening.append(open_batch(*stream[i + 2][0:2]))
                    active.sort(key=lambda w: w[0])
                    still = []
                    for i, work in active:
                        if next(work, active) is not active:
                            still.append((i, work))
                        elif "y" in tiles[stream[i]] and stream[i][2] == TILES - 1 and not tiles[stream[i]].get("fed"):
                            tiles[stream[i]]["fed"] = True
                            fed.append(feed_forward(*stream[i][0:2]))
                    active = still
                    for queue, every in ((opening, 2), (fed, BACK), (preparing, 5)):
                        if queue and now % every == 0 and next(queue[0], active) is active:
                            queue.pop(0)
                    now += 1
                for _ in chain(*fed):
                    pass

                everyone_waits()
                back = sp.dma(x[:, :, :], kept, ch_kept)
                for b in range(BATCH):
                    rows = slice(TILES * b, TILES * (b + 1))
                    x_loaded[b] = dve.do(lambda e: e.tensor_tensor(x[:, rows, :], x[:, rows, :], y[:, rows, :],
                                                                   ALU.add), back)
                everyone_waits()

        def moe_stage():
            with ExitStack() as scope:
                att = FullAttention(scope, "d", DDIM, False, float(1.0 / np.sqrt(np.float32(DDIM))), False)
                side, qkv_width = att.side, D + 2 * DDIM
                ch = channel("d_w")
                raw = sb(scope, "d_raw", [2, D])
                small_raw = sb(scope, "d_small_raw", [2 * D])
                w_qkv, w_out = sb(scope, "d_w_qkv", [qkv_width]), sb(scope, "d_w_out", [D])
                gains = sb(scope, "d_gains", [1])
                sp.dma(raw[:, 0, :], ins["L1_ffn_Wq"], ch)
                sp.dma(raw[:, 1, :], ins["L1_ffn_Wo"], ch)
                sp.dma(small_raw[0:DDIM, 0:D], ins["L1_ffn_Wkc"], ch)
                sp.dma(small_raw[0:DDIM, D:2 * D], ins["L1_ffn_Wvc"], ch)
                loaded = sp.dma(gains[:, :], ins["L1_ffn_g1"].rearrange("(d o) -> d o", o=1), ch)
                act.wait(loaded)
                slot, bank, freed = side.take()
                pe.do(lambda e: e.transpose(bank[:, 0:D], raw[:, 0, :], ident[:, :]), loaded, freed, signal=False)
                for n in range(2):
                    pe.do(lambda e: e.transpose(bank[:, D + DDIM * n:D + DDIM * (n + 1)],
                                                small_raw[0:DDIM, D * n:D * (n + 1)], ident[0:DDIM, 0:DDIM]),
                          signal=False)
                t = pe.do(lambda e: e.transpose(bank[:, qkv_width:qkv_width + D], raw[:, 1, :], ident[:, :]))
                dve.do(lambda e: e.tensor_copy(w_qkv[:, :], bank[:, 0:qkv_width]), t)
                w_ready = dve.do(lambda e: e.tensor_copy(w_out[:, :], bank[:, qkv_width:qkv_width + D]), t)
                side.release(slot, w_ready)
                yn = sb(scope, "d_yn", [TILES, D])
                ynt = sb(scope, "d_ynt", [SEQ])
                qkv = sb(scope, "d_qkv", [TILES, qkv_width])
                free = {}

                def prepare(b, state):
                    tiles = slice(TILES * b, TILES * (b + 1))
                    inner = normalise(x[:, tiles, :], y[:, tiles, :], x_loaded[b], None)
                    yield
                    normed = normalise(y[:, tiles, :], yn, inner, free.get("yn"), rms=True)
                    yield
                    parts = transpose_tiles(yn, ynt, side, normed, free.get("ynt"), evacuate=lambda e, o, i: e.activation(
                        o, i, ACT.Identity, scale=gains[:, 0:1]))
                    free["yn"] = parts[-1]
                    yield
                    for t in range(TILES):
                        slot, bank, freed = side.take()
                        got = pe.do(lambda e: e.matmul(bank[:, 0:qkv_width], ynt[:, P * t:P * (t + 1)], w_qkv[:, :],
                                                       start=True, stop=True), parts, w_ready, freed)
                        end = dve.do(lambda e: e.tensor_copy(qkv[:, t, :], bank[:, 0:qkv_width]), got, free.get("qkv"))
                        side.release(slot, end)
                        yield
                    free["ynt"] = got
                    heads = lambda lo, n: qkv[:, :, lo:lo + n * DDIM].rearrange(
                        "p t (h d) -> p t h d", d=DDIM)
                    qslot, qx, qfreed = att.qx.take()
                    state["qx"], state["qslot"] = qx, qslot
                    z = pool.do(lambda e: e.memset(qx[:, :, :, 3 * DDIM:3 * DDIM + 2].bitcast(F32), 0.0),
                                qfreed, att.cleared)
                    state["q_split"] = [z, att.split(dve, heads(0, DHEADS), qx, "hhl", end, [att.cleared, qfreed])]
                    yield
                    state["k_split"] = att.split(dve, heads(D, 1), att.kx, "hlh", end, [att.cleared, att.kx_free])
                    vslot, v, vfreed = att.v.take()
                    state["v"], state["vslot"] = v, vslot
                    state["v_ready"] = dve.do(lambda e: e.tensor_copy(v[:, :, :, 0:DDIM], heads(D + DDIM, 1)),
                                              end, vfreed, att.cleared)
                    free["qkv"] = state["v_ready"]
                    yield

                def conclude(b, state):
                    for c in range(CHUNKS):
                        slot, bank, freed = side.take()
                        for t in range(TPB):
                            got = pe.do(lambda e: e.matmul(
                                bank[:, P * t:P * (t + 1)], att.ot[:, P * (TPB * c + t):P * (TPB * c + t + 1)],
                                w_out[:, :], start=True, stop=True), att.ot_ready, freed, signal=t == TPB - 1)
                        rows = y[:, TILES * b + TPB * c:TILES * b + TPB * (c + 1), :]
                        end = dve.do(lambda e: e.tensor_tensor(
                            rows, rows, bank.rearrange("p (t d) -> p t d", t=TPB), ALU.add), got)
                        side.release(slot, end)
                        yield
                    att.ot_free = got

                pipeline(att, prepare, conclude)
                everyone_waits()

            with ExitStack() as scope:
                hidden_ring, out_ring, misc = Ring(banks[0:4]), Ring(banks[4:6]), Ring(banks[6:8])
                ch = channel("d_experts")
                n_w = EXPERTS + 1
                raw = [sb(scope, f"d_raw{k}", [n_w, D]) for k in range(3)]
                turned = [sb(scope, f"d_turned{k}", [n_w, D]) for k in range(3)]
                for k, (own, shared) in enumerate((("L1_ffn_eW1", "L1_ffn_sW1"), ("L1_ffn_eW3", "L1_ffn_sW3"),
                                                   ("L1_ffn_eW2", "L1_ffn_sW2"))):
                    sp.dma(raw[k][:, 0:EXPERTS, :], ins[own].rearrange("e a b -> a e b"), ch)
                    sp.dma(raw[k][:, EXPERTS, :], ins[shared], ch)
                router_raw = sb(scope, "d_router_raw", [D])
                router = sb(scope, "d_router", [EXPERTS])
                bias = sb(scope, "d_bias", [EXPERTS])
                gains = sb(scope, "d_gains2", [1])
                numbers = sb(scope, "d_numbers", [EXPERTS])
                sp.dma(router_raw[0:EXPERTS, :], ins["L1_ffn_Wr"], ch)
                sp.dma(bias[:, :], ins["L1_ffn_expert_bias"].partition_broadcast(P), ch)
                sp.dma(numbers[:, :], ins["c_masks"][:, CONST_WIDTH - EXPERTS:CONST_WIDTH], ch)
                loaded = sp.dma(gains[:, :], ins["L1_ffn_g2"].rearrange("(d o) -> d o", o=1), ch)
                slot, bank, freed = misc.take()
                t = pe.do(lambda e: e.transpose(bank[:, 0:EXPERTS], router_raw[0:EXPERTS, :],
                                                ident[0:EXPERTS, 0:EXPERTS]), loaded)
                w_ready = dve.do(lambda e: e.tensor_copy(router[:, :], bank[:, 0:EXPERTS]), t)
                misc.release(slot, w_ready)
                for k in range(3):
                    for lo in range(0, n_w, 4):
                        hi = min(n_w, lo + 4)
                        slot, bank, freed = misc.take()
                        for n in range(lo, hi):
                            t = pe.do(lambda e: e.transpose(bank[:, D * (n - lo):D * (n - lo + 1)], raw[k][:, n, :],
                                                            ident[:, :]), freed, signal=n == hi - 1)
                        w_ready = dve.do(lambda e: e.tensor_copy(
                            turned[k][:, lo:hi, :].rearrange("p a b -> p (a b)"), bank[:, 0:D * (hi - lo)]), t)
                        misc.release(slot, w_ready)
                w1t, w3t, w2t = turned
                yn = Ring([sb(scope, f"d_yn{n}", [TILES, D]) for n in range(2)])
                ynt = Ring([sb(scope, f"d_ynt{n}", [SEQ]) for n in range(2)])
                gate = Ring([sb(scope, f"d_gate{n}", [BANK]) for n in range(2)])
                hid = Ring([sb(scope, f"d_hid{n}", [BANK]) for n in range(2)])
                part = Ring([sb(scope, f"d_part{n}", [BANK]) for n in range(2)])
                te = lambda name, n=EXPERTS, dt=F32: sb(scope, f"d_{name}", [TILES, n], dt)
                logits, weights, best, chosen = te("logits"), te("weights"), te("best"), te("chosen")
                where = te("where", EXPERTS, U32)
                second, combine = te("second"), Ring([te(f"combine{n}") for n in range(2)])
                one = sb(scope, "d_one", [5, TILES])
                act.wait(loaded)
                routed = None

                for b in range(BATCH):
                    rows = y[:, TILES * b:TILES * (b + 1), :]
                    nslot, yb, nfreed = yn.take()
                    normed = normalise(rows, yb, None, nfreed, rms=True)
                    tslot, yt, tfreed = ynt.take()
                    ready = transpose_tiles(yb, yt, misc, normed, tfreed, evacuate=lambda e, o, i: e.activation(
                        o, i, ACT.Identity, scale=gains[:, 0:1]))
                    yn.release(nslot, ready)
                    slot, bank, freed = misc.take()
                    for t in range(TILES):
                        got = pe.do(lambda e: e.matmul(bank[:, EXPERTS * t:EXPERTS * (t + 1)], yt[:, P * t:P * (t + 1)],
                                                       router[:, :], start=True, stop=True),
                                    ready, w_ready, freed, signal=t == TILES - 1)
                    scores = bank[:, 0:EXPERTS * TILES].rearrange("p (t e) -> p t e", t=TILES)
                    across = lambda ap: bcast(ap, 2, EXPERTS)
                    a = dve.do(lambda e: e.tensor_tensor(logits[:], scores, bcast(bias[:, :], 1, TILES), ALU.add),
                               got, routed)
                    misc.release(slot, a)
                    a = dve.do(lambda e: e.tensor_reduce(one[:, 0, :], logits[:], AX.X, ALU.max), a)
                    a = dve.do(lambda e: e.tensor_tensor(logits[:], logits[:], across(one[:, 0, :]), ALU.subtract), a)
                    a = act.do(lambda e: e.activation(weights[:], logits[:], ACT.Exp), a)
                    a = dve.do(lambda e: e.tensor_reduce(one[:, 1, :], weights[:], AX.X, ALU.add), a)
                    a = dve.do(lambda e: e.reciprocal(one[:, 2, :], one[:, 1, :]), a)
                    a = dve.do(lambda e: e.tensor_tensor(weights[:], weights[:], across(one[:, 2, :]), ALU.mult), a)
                    for t in range(TILES):
                        m = dve.do(lambda e: e.max(best[:, t, :], weights[:, t, :]), a)
                    for t in range(TILES):
                        n = dve.do(lambda e: e.max_index(where[:, t, :], best[:, t, :], weights[:, t, :]), m)
                    n = dve.do(lambda e: e.tensor_copy(chosen[:], where[:]), n)
                    a = dve.do(lambda e: e.tensor_tensor(one[:, 3, :], best[:, :, 1], best[:, :, 0], ALU.subtract), m)
                    a = act.do(lambda e: e.activation(one[:, 4, :], one[:, 3, :], ACT.Exp), a)
                    a = dve.do(lambda e: e.tensor_scalar(one[:, 3, :], one[:, 4, :], 1.0, None, ALU.add), a)
                    a = dve.do(lambda e: e.reciprocal(one[:, 2, :], one[:, 3, :]), a)
                    a = dve.do(lambda e: e.tensor_tensor(one[:, 1, :], one[:, 4, :], one[:, 2, :], ALU.mult), a)
                    cslot, share, cfreed = combine.take()
                    each = bcast(numbers[:, :], 1, TILES)
                    f = dve.do(lambda e: e.tensor_tensor(share[:], each, across(chosen[:, :, 0]), ALU.is_equal),
                               n, cfreed)
                    g = dve.do(lambda e: e.tensor_tensor(second[:], each, across(chosen[:, :, 1]), ALU.is_equal), n)
                    f = dve.do(lambda e: e.tensor_tensor(share[:], share[:], across(one[:, 2, :]), ALU.mult), f, a)
                    g = dve.do(lambda e: e.tensor_tensor(second[:], second[:], across(one[:, 1, :]), ALU.mult), g, a)
                    routed = dve.do(lambda e: e.tensor_tensor(share[:], share[:], second[:], ALU.add), f, g)
                    summed = [normed] * CHUNKS
                    for x_no in range(n_w):
                        for c in range(CHUNKS):
                            cols = slice(BANK * c, BANK * (c + 1))
                            s1, bank1, f1 = hidden_ring.take()
                            s3, bank3, f3 = hidden_ring.take()
                            g1 = pe.do(lambda e: e.matmul(bank1, w1t[:, x_no, :], yt[:, cols], start=True, stop=True),
                                       ready, w_ready, f1)
                            g3 = pe.do(lambda e: e.matmul(bank3, w3t[:, x_no, :], yt[:, cols], start=True, stop=True), f3)
                            gs, gt, gf = gate.take()
                            opened = act.do(lambda e: e.activation(gt[:, :], bank1, ACT.Silu), g1, gf)
                            hidden_ring.release(s1, opened)
                            hs, ht, hf = hid.take()
                            made = dve.do(lambda e: e.tensor_tensor(ht[:, :], gt[:, :], bank3, ALU.mult), g3, opened, hf)
                            hidden_ring.release(s3, made)
                            gate.release(gs, made)
                            os, bank, of = out_ring.take()
                            for t in range(TPB):
                                got = pe.do(lambda e: e.matmul(bank[:, D * t:D * (t + 1)], ht[:, P * t:P * (t + 1)],
                                                               w2t[:, x_no, :], start=True, stop=True),
                                            made, of, signal=t == TPB - 1)
                            hid.release(hs, got)
                            by_tile = bank.rearrange("p (t d) -> p t d", t=TPB)
                            tiles = slice(TPB * c, TPB * (c + 1))
                            if x_no < EXPERTS:
                                ps, pt, pf = part.take()
                                pt = pt[:, :].rearrange("p (t d) -> p t d", t=TPB)
                                scaled = dve.do(lambda e: e.tensor_tensor(
                                    pt, by_tile, bcast(share[:, tiles, x_no], 2, D), ALU.mult), got, routed, pf)
                                out_ring.release(os, scaled)
                                summed[c] = pool.do(lambda e: e.tensor_tensor(
                                    rows[:, tiles, :], rows[:, tiles, :], pt, ALU.add), scaled, summed[c])
                                part.release(ps, summed[c])
                            else:
                                summed[c] = dve.do(lambda e: e.tensor_tensor(
                                    rows[:, tiles, :], rows[:, tiles, :], by_tile, ALU.add), got, summed[c])
                                out_ring.release(os, summed[c])
                    ynt.release(tslot, got)
                    combine.release(cslot, scaled)
                    batch = slice(TILES * b, TILES * (b + 1))
                    x_loaded[b] = pool.do(lambda e: e.tensor_tensor(x[:, batch, :], x[:, batch, :], y[:, batch, :],
                                                                    ALU.add), summed)

        if "A" in stages:
            mha_stage("a", ("L0_attn_wq", "L0_attn_wk", "L0_attn_wv", "L0_attn_wo"),
                      ("L0_attn_bq", "L0_attn_bk", "L0_attn_bv", "L0_attn_bo"), 0, False)
        if "B" in stages:
            local_stage()
        if "C" in stages:
            mha_stage("c", ("L1_attn_W_Q", "L1_attn_W_K", "L1_attn_W_V", "L1_attn_W_O"), (), 16, True)

        if "D" in stages:
            moe_stage()

        ch_out = channel("out")
        stored = sp.dma(out.rearrange("b (t p) d -> p (b t) d", p=P), x[:, :, :], ch_out,
                        dve.last(), pool.last(), act.last())
        sp.wait(stored)


def kernel(**inputs):
    import concourse.bacc as bacc
    from concourse.bass_utils import run_bass_kernel_spmd

    nc = bacc.Bacc("TRN2", target_bir_lowering=False, num_devices=1)
    small, local = rotary_constants()
    given = {name: np.ascontiguousarray(value) for name, value in inputs.items()}
    given.update(c_small=small, c_local=local, c_masks=mask_constants())
    arrays = {f"in_{name}": value for name, value in given.items()}
    ins = {name: nc.dram_tensor(f"in_{name}", value.shape, mybir.dt.from_np(value.dtype),
                                kind="ExternalInput").ap() for name, value in given.items()}
    out = nc.dram_tensor("out_x", (BATCH, SEQ, D), F32, kind="ExternalOutput").ap()
    build(nc, ins, out)
    return run_bass_kernel_spmd(nc, [arrays], core_ids=[0]).results[0]["out_x"]
```

```python
from contextlib import ExitStack

import numpy as np

import concourse.bass as bass
from concourse import mybir

F32 = mybir.dt.float32
F32R = mybir.dt.float32r
BF16 = mybir.dt.bfloat16
U32 = mybir.dt.uint32
I32 = mybir.dt.int32
ACT = mybir.ActivationFunctionType
ALU = mybir.AluOpType
AX = mybir.AxisListType

P = 128
D = 128
BATCH, SEQ = 4, 1024
TILES = SEQ // P
NT = BATCH * TILES
BANK = 512
CHUNKS = SEQ // BANK
TPB = BANK // P

HEADS_PER_UNIT = 4
ROWS = P // HEADS_PER_UNIT
EPS_LN, EPS_RMS = 1e-5, 1e-6
PAUSE1, PAUSE2, CLOSED, ENDING, PREPARE = 2, 4, 3, 16, 24
MASKED = -1.0e30

DEPTH, LHEADS, LDIM, WINDOW = 6, 16, 64, 32
INNER = LHEADS * LDIM
FF = int(D * 4 * 2 / 3)
QK_SCALE = 8.0
WPT = P // WINDOW
HPC = BANK // LDIM
PAIRS = LHEADS // 2
ROUNDS, LAGS = 12, (0, 14, 23, 29)
FED_EVERY, OPENING_EVERY, PREPARING_EVERY = (3, 0), (4, 2), (6, 4)
FBLOCKS = [(k, min(P, FF - k)) for k in range(0, FF, P)]

DHEADS, DDIM = 4, 32
EXPERTS = 8
CONST_WIDTH = 3 * P + 4 * WINDOW + EXPERTS


class Engine:

    def __init__(self, queue, semaphore):
        self.queue, self.semaphore, self.count, self.passed = queue, semaphore, 0, {}

    def wait(self, *events):
        for event in events:
            if isinstance(event, list):
                self.wait(*event)
            elif event is not None and self.passed.get(event[0].name, 0) < event[1]:
                self.passed[event[0].name] = event[1]
                self.queue.wait_ge(event[0], event[1])

    def do(self, instruction, *events, signal=True):
        self.wait(*events)
        made = instruction(self.queue)
        if not signal:
            return None
        self.count += 1
        made.then_inc(self.semaphore, 1)
        return self.semaphore, self.count

    def dma(self, out, in_, channel, *events):
        self.wait(*events)
        channel.count += 16
        self.queue.dma_start(out, in_).then_inc(channel.semaphore, 16)
        return channel.semaphore, channel.count

    def last(self):
        return (self.semaphore, self.count) if self.count else None


class Channel:

    def __init__(self, semaphore):
        self.semaphore, self.count = semaphore, 0


class Ring:

    def __init__(self, views):
        self.views, self.free, self.at = views, [[] for _ in views], -1

    def take(self):
        self.at = (self.at + 1) % len(self.views)
        freed, self.free[self.at] = self.free[self.at], None
        assert freed is not None, "a buffer is taken before its last use is queued"
        return self.at, self.views[self.at], freed

    def release(self, slot, *events):
        self.free[slot] = list(events)


def weave(main, steps, *sides):
    taken = [0] * len(sides)
    for n, _ in enumerate(main, 1):
        for k, (side, count) in enumerate(sides):
            while taken[k] * steps < n * count:
                next(side, None)
                taken[k] += 1


def run(steps):
    for _ in steps:
        pass


def chain(*parts):
    for part in parts:
        yield from part


def bcast(ap, axis, n):
    shape = list(ap.shape)
    return ap.unsqueeze(axis).to_broadcast(shape[:axis] + [n] + shape[axis:])


def rotary_constants():
    f = np.float32
    t = np.arange(SEQ, dtype=f)
    theta = f(10000.0) ** (f(-2.0) * np.arange(4, dtype=f) / f(8))
    ang = t[:, None] * theta[None, :]
    cos_a, sin_a = np.repeat(np.cos(ang), 2, -1), np.repeat(np.sin(ang), 2, -1)
    theta = f(1.0) / f(10000.0) ** (np.arange(0, 8, 2, dtype=f) / f(8))
    ang = np.concatenate([t[:, None] * theta[None, :]] * 2, -1)
    cos_c, sin_c = np.cos(ang), np.sin(ang)
    sign = np.array([-1] * 4 + [1] * 4, f)
    small = np.concatenate([cos_a, sin_a * sign, cos_c, sin_c * sign], -1)
    half = np.arange(0, LDIM, 2, dtype=f)
    freqs = t[:, None] * (f(1.0) / f(10000.0) ** (half / f(LDIM)))[None, :]
    base = (half + f(0.4 * LDIM)) / f(1.4 * LDIM)
    power = (t - SEQ // 2) / f(WINDOW // 2)
    scale = base[None, :] ** power[:, None]
    cos, sin = np.cos(freqs), np.sin(freqs)
    local = np.concatenate([cos * scale * f(QK_SCALE), sin * scale * f(QK_SCALE),
                            cos / scale, sin / scale], -1)
    by_tile = lambda a: np.ascontiguousarray(
        a.astype(f).reshape(TILES, P, -1).transpose(1, 0, 2).reshape(P, -1))
    return by_tile(small), by_tile(local)


def mask_constants():
    i = np.arange(P)
    causal_qk = np.where(i[:, None] < i[None, :], MASKED, 0.0)
    q, k = np.arange(WINDOW)[:, None], np.arange(2 * WINDOW)[None, :] - WINDOW
    window = np.where((q < k) | (q > k + WINDOW), MASKED, 0.0)
    first = np.where(k < 0, MASKED, window)
    usual = np.tile(window, (WPT, 1))
    opening = np.concatenate([first] + [window] * (WPT - 1), 0)
    numbers = np.tile(np.arange(EXPERTS), (P, 1))
    return np.concatenate([np.eye(P), causal_qk, causal_qk.T, usual, opening, numbers], 1).astype(np.float32)


def build(nc, ins, out, stages="ABCD"):
    with ExitStack() as whole:
        enter = whole.enter_context
        pe = Engine(nc.tensor, enter(nc.semaphore("tensor_done")))
        act = Engine(nc.scalar, enter(nc.semaphore("scalar_done")))
        dve = Engine(nc.vector, enter(nc.semaphore("vector_done")))
        pool = Engine(nc.gpsimd, enter(nc.semaphore("gpsimd_done")))
        sp = Engine(nc.sync, enter(nc.semaphore("sync_done")))

        def channel(name):
            return Channel(enter(nc.semaphore(f"dma_{name}")))

        def sb(scope, name, shape, dt=F32):
            return scope.enter_context(nc.sbuf_tensor(name, [P] + list(shape), dt))

        def everyone_waits():
            events = [e.last() for e in (pe, act, dve, pool)]
            for e in (pe, act, dve, pool, sp):
                e.wait(*events)

        psum = enter(nc.psum_tensor("psum", [P, 8, BANK], F32))
        banks = [psum[:, n, :] for n in range(8)]

        x = sb(whole, "x", [NT, D])
        y = sb(whole, "y", [NT, D])
        ident = sb(whole, "ident", [P])
        ident_bf = sb(whole, "ident_bf", [P], BF16)
        ones = sb(whole, "ones", [P])
        moments = sb(whole, "moments", [2, TILES, 6])
        mean_var = sb(whole, "mean_var", [2, TILES, 2])
        spread = sb(whole, "spread", [2, TILES, 2])

        ch_x = [channel(f"x{b}") for b in range(BATCH)]
        ch_const = channel("constants")
        masks_f = y[:, :, :].rearrange("p t d -> p (t d)")[:, 0:2 * P + 4 * WINDOW]
        masks = sb(whole, "masks", [2 * P + 4 * WINDOW], BF16)
        causal_qk, causal_kq = masks[:, 0:P], masks[:, P:2 * P]
        window_mask, opening_mask = (masks[:, 2 * P + 2 * WINDOW * k:2 * P + 2 * WINDOW * (k + 1)]
                                     for k in range(2))
        small_rot = sb(whole, "small_rot", [TILES, 32])
        sp.dma(ident[:, :], ins["c_masks"][:, 0:P], ch_const)
        x_in = ins["L0_attn_x"].rearrange("b (t p) d -> b p t d", p=P)
        x_loaded = [sp.dma(x[:, TILES * b:TILES * (b + 1), :], x_in[b], ch_x[b]) for b in range(BATCH)]
        sp.dma(masks_f, ins["c_masks"][:, P:CONST_WIDTH - EXPERTS], ch_const)
        const_loaded = sp.dma(small_rot[:, :, :], ins["c_small"].rearrange("p (t c) -> p t c", t=TILES),
                              ch_const)
        ones_set = pool.do(lambda e: e.memset(ones[:, :], 1.0))
        dve.do(lambda e: e.tensor_copy(masks[:, :], masks_f), const_loaded)
        const_ready = dve.do(lambda e: e.tensor_copy(ident_bf[:, :], ident[:, :]))
        act.wait(ones_set)
        pe.wait(const_loaded, const_ready, ones_set)

        def inverse_root(engine, dst, src, tmp, ready):
            got = engine.do(lambda e: e.tensor_scalar(
                dst.bitcast(I32), src.bitcast(I32), -0.5, float(0x5f3759df), ALU.mult, ALU.add), ready)
            for _ in range(3):
                got = engine.do(lambda e: e.tensor_tensor(tmp, dst, dst, ALU.mult), got)
                got = engine.do(lambda e: e.scalar_tensor_tensor(
                    out=tmp, in0=tmp, scalar=-0.5, in1=src, op0=ALU.mult, op1=ALU.mult), got)
                got = engine.do(lambda e: e.scalar_tensor_tensor(
                    out=dst, in0=tmp, scalar=1.5, in1=dst, op0=ALU.add, op1=ALU.mult), got)
            return got

        norm_slot = Ring([0, 1])

        def normalise(*args, **kwargs):
            steps = normalise_steps(*args, **kwargs)
            while True:
                try:
                    next(steps)
                except StopIteration as stop:
                    return stop.value

        def normalise_steps(src, dst, ready, dst_free, rms=False):
            slot, _, freed = norm_slot.take()
            mo, mv, sd = moments[:, slot], mean_var[:, slot], spread[:, slot]
            for t in range(TILES):
                seen = dve.do(lambda e, t=t: e.bn_stats(mo[:, t, :], src[:, t, :]), ready, freed)
            yield
            for t in range(TILES):
                got = dve.do(lambda e, t=t: e.bn_aggr(mv[:, t, :], mo[:, t, :]), seen)
            if rms:
                got = dve.do(lambda e: e.tensor_tensor(sd[:, :, 0], mv[:, :, 0], mv[:, :, 0], ALU.mult), got)
                got = dve.do(lambda e: e.tensor_tensor(mv[:, :, 1], mv[:, :, 1], sd[:, :, 0], ALU.add), got)
            got = dve.do(lambda e: e.tensor_scalar(
                mv[:, :, 1], mv[:, :, 1], EPS_RMS if rms else EPS_LN, None, ALU.add), got)
            inv = inverse_root(dve, sd[:, :, 1], mv[:, :, 1], sd[:, :, 0], got)
            yield
            for t in range(TILES):
                if rms:
                    end = dve.do(lambda e, t=t: e.tensor_scalar(
                        dst[:, t, :], src[:, t, :], sd[:, t, 1:2], None, ALU.mult), inv, dst_free)
                else:
                    end = dve.do(lambda e, t=t: e.tensor_scalar(
                        dst[:, t, :], src[:, t, :], mv[:, t, 0:1], sd[:, t, 1:2],
                        ALU.subtract, ALU.mult), inv, dst_free)
            norm_slot.release(slot, end)
            return end

        def transpose_tiles(src, dst, ring, ready, dst_free, evacuate=None, engine=act):
            done = []
            for c in range(CHUNKS):
                slot, bank, freed = ring.take()
                for t in range(TPB):
                    turned = pe.do(lambda e, t=t: e.transpose(
                        bank[:, P * t:P * (t + 1)], src[:, TPB * c + t, :], ident[:, :]),
                        ready, freed, signal=t == TPB - 1)
                move = evacuate or (lambda e, o, i: e.copy(o, i) if engine is act else e.tensor_copy(o, i))
                got = engine.do(lambda e: move(e, dst[:, BANK * c:BANK * (c + 1)], bank), turned, dst_free)
                ring.release(slot, got)
                done.append(got)
            return done

        def transposed_weight(scope, name, source, rows, ring, ch):
            raw = sb(scope, f"{name}_raw", [D])
            turned = sb(scope, name, [rows])
            loaded = sp.dma(raw[0:rows, :], source, ch)
            slot, bank, freed = ring.take()
            t = pe.do(lambda e: e.transpose(bank[:, 0:rows], raw[0:rows, :], ident[0:rows, 0:rows]), loaded, freed)
            got = dve.do(lambda e: e.tensor_copy(turned[:, :], bank[:, 0:rows]), t)
            ring.release(slot, got)
            return turned, got

        class FullAttention:

            def __init__(self, scope, name, dim, causal, scale, own_keys):
                self.dim, self.causal, self.scale, self.own_keys = dim, causal, scale, own_keys
                self.width = ROWS if own_keys else P
                self.nq = 1 if own_keys else HEADS_PER_UNIT
                self.units = 16 // HEADS_PER_UNIT if own_keys else 1
                heads = self.units * HEADS_PER_UNIT
                kheads = heads if own_keys else 1
                nk = HEADS_PER_UNIT if own_keys else 1
                w = self.width
                self.qx = Ring([sb(scope, f"{name}_qx{n}", [TILES, heads, w], F32R) for n in range(1)])
                self.kx = sb(scope, f"{name}_kx", [TILES, kheads, w], F32R)
                self.q1 = Ring([sb(scope, f"{name}_q1_{n}", [self.nq, SEQ], F32R) for n in range(1)])
                self.q2 = Ring([sb(scope, f"{name}_q2_{n}", [self.nq, SEQ], F32R) for n in range(2)])
                self.kt = Ring([sb(scope, f"{name}_kt{n}", [nk, SEQ], F32R) for n in range(2)])
                self.top2 = sb(scope, f"{name}_top2", [TILES, HEADS_PER_UNIT, CHUNKS])
                self.top = sb(scope, f"{name}_top", [TILES, HEADS_PER_UNIT])
                self.v = Ring([sb(scope, f"{name}_v{n}", [TILES, kheads, ROWS]) for n in range(2 if own_keys else 3)])
                self.prob = Ring([sb(scope, f"{name}_prob{n}", [BANK]) for n in range(8)])
                self.ot = sb(scope, f"{name}_ot", [SEQ])
                self.ot_free = self.rsum_free = None
                self.o = sb(scope, f"{name}_o", [TILES, D])
                self.o_free = None
                if not own_keys:
                    self.sums = sb(scope, f"{name}_sums", [SEQ])
                if own_keys:
                    self.score_banks, self.side = Ring(banks[0:3]), Ring(banks[3:6])
                else:
                    self.score_banks, self.side, self.sum_banks = Ring(banks[0:2]), Ring(banks[2:4]), banks[4:6]
                self.out_banks = banks[6:8]
                self.out_free = None
                self.top_free = None
                self.pending = None
                zeroed = []
                for t in self.qx.views + [self.kx] + self.kt.views:
                    zeroed.append(pool.do(lambda e, t=t: e.memset(t[:].bitcast(F32), 0.0)))
                for t in self.v.views:
                    zeroed.append(pool.do(lambda e, t=t: e.memset(t[:], 0.0)))
                z = zeroed[-1]
                mid = 3 * dim
                z = pool.do(lambda e: e.memset(self.kx[:, :, :, mid:mid + 2].bitcast(F32), 1.0), z)
                if own_keys:
                    for t in self.v.views:
                        z = pool.do(lambda e, t=t: e.memset(t[:, :, :, dim:dim + 1], 1.0), z)
                self.cleared = z
                self.kx_free = None

            def split(self, engine, src, dst, order, ready, freed):
                d = self.dim
                high = order.index("h")
                first = engine.do(lambda e: e.tensor_copy(dst[:, :, :, high * d:(high + 1) * d], src), ready, freed)
                for n, part in enumerate(order):
                    if n == high:
                        continue
                    o = dst[:, :, :, n * d:(n + 1) * d]
                    h = dst[:, :, :, high * d:(high + 1) * d].bitcast(F32)
                    if part == "h":
                        end = engine.do(lambda e, o=o: e.tensor_copy(o, h), first)
                    else:
                        end = engine.do(lambda e, o=o: e.tensor_tensor(o, src, h, ALU.subtract), first)
                return end

            def turn(self, src, unit, dst, ready, dst_free, blocks):
                for n in range(blocks):
                    for c in range(CHUNKS):
                        slot, bank, freed = self.side.take()
                        for t in range(TPB):
                            lo = unit * HEADS_PER_UNIT if self.own_keys else n
                            hi = lo + (HEADS_PER_UNIT if self.own_keys else 1)
                            turned = pe.do(lambda e, t=t, lo=lo, hi=hi: e.transpose(
                                bank[:, P * t:P * (t + 1)],
                                src[:, TPB * c + t, lo:hi, :].rearrange("p h w -> p (h w)").bitcast(F32),
                                ident[:, :]), ready, freed, signal=t == TPB - 1)
                        yield n, c, slot, bank, turned

            def unit_first(self, b, unit, state):
                qx, kx = state["qx"], self.kx
                kslot, kt, kfreed = self.kt.take()
                for n, c, slot, bank, turned in self.turn(kx, unit, kt, state["k_split"], None, 1):
                    cols = slice(BANK * c, BANK * (c + 1))
                    if self.own_keys:
                        for g in range(HEADS_PER_UNIT):
                            rows = slice(ROWS * g, ROWS * (g + 1))
                            end = act.do(lambda e, g=g, rows=rows: e.copy(kt[rows, g, cols], bank[rows, :]),
                                         turned, kfreed, self.cleared)
                    else:
                        end = act.do(lambda e: e.copy(kt[:, 0, cols], bank), turned, kfreed, self.cleared)
                    self.side.release(slot, end)
                    yield
                k_ready = end
                self.kx_free = turned
                q1slot, q1, q1freed = self.q1.take()
                for n, c, slot, bank, turned in self.turn(qx, unit, q1, state["q_split"], None, self.nq):
                    end = act.do(lambda e: e.copy(q1[:, n, BANK * c:BANK * (c + 1)], bank), turned, q1freed)
                    self.side.release(slot, end)
                    yield
                q1_ready, turned_once = end, turned
                for _ in range(PAUSE1):
                    yield
                for t in range(TILES):
                    for g in range(HEADS_PER_UNIT):
                        lhs = q1[:, g if self.nq > 1 else 0, P * t:P * (t + 1)]
                        width = (t + 1) * P if self.causal else SEQ
                        for c in range(-(-width // BANK)):
                            hi = min(width, BANK * (c + 1))
                            n = hi - BANK * c
                            slot, bank, freed = self.side.take()
                            diagonal = self.causal and hi == width
                            rhs = kt[:, g if self.own_keys else 0, BANK * c:hi]
                            if diagonal:
                                pe.do(lambda e: e.matmul(
                                    bank[:, n - P:n], ident_bf[:, :], causal_qk, start=True, stop=False,
                                    skip_group_check=True), freed, signal=False)
                            got = pe.do(lambda e: e.matmul(
                                bank[:, 0:n], lhs, rhs, start=not diagonal, stop=True, skip_group_check=diagonal),
                                k_ready, q1_ready, freed)
                            end = dve.do(lambda e, n=n: e.tensor_reduce(
                                self.top2[:, t, g, c:c + 1], bank[:, 0:n], AX.X, ALU.max), got, self.top_free)
                            self.side.release(slot, end)
                            yield
                        if self.causal and c + 1 < CHUNKS:
                            end = dve.do(lambda e: e.tensor_copy(self.top2[:, t, g, 1:2], self.top2[:, t, g, 0:1]), end)
                self.q1.release(q1slot, got)
                top, heads = self.top, slice(unit * HEADS_PER_UNIT, (unit + 1) * HEADS_PER_UNIT)
                m = dve.do(lambda e: e.tensor_reduce(top[:, :, :], self.top2[:, :, :, :], AX.X, ALU.max, negate=True), end)
                mh = qx[:, :, heads, 3 * self.dim]
                ml = qx[:, :, heads, 3 * self.dim + 1]
                m = dve.do(lambda e: e.tensor_copy(mh, top[:, :, :]), m, turned_once)
                m = dve.do(lambda e: e.tensor_tensor(ml, top[:, :, :], mh.bitcast(F32), ALU.subtract), m)
                self.top_free = m
                for _ in range(PAUSE2):
                    yield
                q2slot, q2, q2freed = self.q2.take()
                for n, c, slot, bank, turned in self.turn(qx, unit, q2, m, None, self.nq):
                    end = act.do(lambda e: e.copy(q2[:, n, BANK * c:BANK * (c + 1)], bank), turned, q2freed)
                    self.side.release(slot, end)
                    yield
                if unit == self.units - 1:
                    self.qx.release(state["qslot"], turned)
                state[unit] = (kslot, kt, k_ready, q2slot, q2, end)

            def unit_second(self, b, unit, state):
                kslot, kt, k_ready, q2slot, q2, q_ready = state.pop(unit)
                v, v_ready = state["v"], state["v_ready"]
                started = set()
                waiting = []

                def values(group):
                    for g, c, lo, pslot, prob, ready, kt_i in group:
                        head = (unit * HEADS_PER_UNIT + g) if self.own_keys else 0
                        first = (g, c) not in started
                        started.add((g, c))
                        last = kt_i == (min(TILES, TPB * (c + 1)) - 1 if self.causal else TILES - 1)
                        o = self.out_banks[c][ROWS * g:ROWS * (g + 1), lo:BANK]
                        done = pe.do(lambda e, o=o, kt_i=kt_i, head=head, prob=prob, lo=lo, first=first, last=last: e.matmul(
                            o, v[:, kt_i, head, :], prob[:, lo:BANK], start=first, stop=last,
                            skip_group_check=True, tile_position=(0, ROWS * g)), ready, v_ready, self.out_free)
                        if not self.own_keys:
                            s = self.sum_banks[c][ROWS * g:ROWS * (g + 1), lo:BANK]
                            done = pe.do(lambda e, s=s, prob=prob, lo=lo, first=first, last=last: e.matmul(
                                s, ones[:, 0:ROWS], prob[:, lo:BANK], start=first, stop=last,
                                skip_group_check=True, tile_position=(0, ROWS * g)))
                        self.prob.release(pslot, done)
                    return done

                for kt_i in range(TILES):
                    for c in range(CHUNKS):
                        lo = max(0, kt_i * P - c * BANK) if self.causal else 0
                        if lo >= BANK:
                            continue
                        group = []
                        for g in range(HEADS_PER_UNIT):
                            slot, bank, freed = self.score_banks.take()
                            lhs = kt[:, g if self.own_keys else 0, P * kt_i:P * (kt_i + 1)]
                            rhs = q2[:, g if self.nq > 1 else 0, BANK * c + lo:BANK * (c + 1)]
                            diagonal = self.causal and kt_i * P >= c * BANK
                            if diagonal:
                                pe.do(lambda e: e.matmul(
                                    bank[:, lo:lo + P], ident_bf[:, :], causal_kq, start=True, stop=False,
                                    skip_group_check=True), freed, signal=False)
                            got = pe.do(lambda e: e.matmul(
                                bank[:, lo:BANK], lhs, rhs, start=not diagonal, stop=True, skip_group_check=diagonal),
                                k_ready, q_ready, freed)
                            pslot, prob, pfreed = self.prob.take()
                            ready = act.do(lambda e, bank=bank, prob=prob, lo=lo: e.activation(
                                prob[:, lo:BANK], bank[:, lo:BANK], ACT.Exp, scale=self.scale), got, pfreed)
                            self.score_banks.release(slot, ready)
                            group.append((g, c, lo, pslot, prob, ready, kt_i))
                            yield
                        waiting.append(group)
                        if len(waiting) > 1:
                            values(waiting.pop(0))
                        else:
                            self.close()
                self.kt.release(kslot, got)
                self.q2.release(q2slot, got)

                def last_values():
                    done = values(waiting.pop(0))
                    if unit == self.units - 1:
                        self.v.release(state["vslot"], done)
                    self.finish(done)
                self.pending = last_values

            def close(self):
                if self.pending:
                    self.pending()
                self.pending = None

            def finish(self, done):
                ot = self.ot
                for c in range(CHUNKS):
                    if self.own_keys:
                        end = dve.do(lambda e, c=c: e.tensor_copy(ot[:, BANK * c:BANK * (c + 1)], self.out_banks[c]),
                                     done, self.ot_free)
                    else:
                        cols = slice(BANK * c, BANK * (c + 1))
                        act.do(lambda e: e.copy(self.sums[:, cols], self.sum_banks[c]), done, self.ot_free)
                        end = act.do(lambda e: e.copy(ot[:, cols], self.out_banks[c]))
                self.out_free = end
                if not self.own_keys:
                    for c in range(CHUNKS):
                        cols = slice(BANK * c, BANK * (c + 1))
                        r = dve.do(lambda e: e.reciprocal(self.sums[:, cols], self.sums[:, cols]), end)
                        self.ot_ready = dve.do(lambda e: e.tensor_tensor(
                            ot[:, cols], ot[:, cols], self.sums[:, cols], ALU.mult), r)
                else:
                    self.ot_ready = end

            def turn_back(self, unit):
                for _ in range(CLOSED):
                    yield
                assert self.pending is None
                if not self.own_keys:
                    return
                ot, o = self.ot, self.o
                for c in range(CHUNKS):
                    slot, bank, freed = self.side.take()
                    for t in range(TPB):
                        turned = pe.do(lambda e, t=t, c=c: e.transpose(
                            bank[:, P * t:P * (t + 1)], ot[:, P * (TPB * c + t):P * (TPB * c + t + 1)],
                            ident[:, :]), self.ot_ready, freed, signal=t == TPB - 1)
                    heads = bank.rearrange("p (t g w) -> p t g w", t=TPB, g=HEADS_PER_UNIT)
                    r = dve.do(lambda e: e.reciprocal(self.rsum[:, :, :], heads[:, :, :, self.dim]), turned, self.rsum_free)
                    dst = o[:, TPB * c:TPB * (c + 1), unit * 32:(unit + 1) * 32].rearrange(
                        "p t (g d) -> p t g d", g=HEADS_PER_UNIT)
                    got = dve.do(lambda e: e.tensor_tensor(
                        dst, heads[:, :, :, 0:self.dim], bcast(self.rsum[:, :, :], 3, self.dim), ALU.mult),
                        r, self.o_free)
                    self.side.release(slot, got)
                    self.rsum_free = got
                    yield
                self.ot_free = turned
                self.o_ready = got

        def pipeline(att, prepare, split, conclude):
            states = [dict() for _ in range(BATCH)]
            order = [(b, u) for b in range(BATCH) for u in range(att.units)]

            scores = sum(HEADS_PER_UNIT * (-(-(t + 1) * P // BANK) if att.causal else CHUNKS)
                         for t in range(TILES))
            steps = scores + CHUNKS * (1 + 2 * att.nq) + PAUSE1 + PAUSE2
            ahead = min(3, att.units)
            run(prepare(0, states[0]))
            split(0, states[0])
            if att.units == 1:
                run(prepare(1, states[1]))
            run(att.unit_first(0, 0, states[0]))
            ending = preparing = iter(())
            for i, (b, u) in enumerate(order):
                coming = b + (1 if att.units > 1 else 2)
                if u == 0 and coming < BATCH:
                    preparing = prepare(coming, states[coming])
                if i + 1 < len(order):
                    nb, nu = order[i + 1]
                    if nu == 0:
                        if att.units > 1:
                            run(preparing)
                        split(nb, states[nb])
                    nxt = att.unit_first(nb, nu, states[nb])
                else:
                    nxt = iter(())
                weave(att.unit_second(b, u, states[b]), scores, (nxt, steps), (ending, ENDING),
                      (preparing, -(-PREPARE // ahead)))
                run(nxt)
                run(ending)
                if att.units == 1:
                    run(preparing)
                ending = att.turn_back(u)
                if u == att.units - 1:
                    ending = chain(ending, conclude(b, states[b]))
            att.close()
            run(ending)

        def mha_stage(name, w_names, biases, rot, causal):
            with ExitStack() as scope:
                att = FullAttention(scope, name, 8, causal, float(1.0 / np.sqrt(np.float32(8))), True)
                side = att.side
                att.rsum = sb(scope, f"{name}_rsum", [TPB, HEADS_PER_UNIT])
                ch = channel(f"{name}_w")
                w_qkv = sb(scope, f"{name}_w_qkv", [3 * D])
                w_out = sb(scope, f"{name}_w_out", [D])
                raw = sb(scope, f"{name}_raw", [4, D])
                for n, w in enumerate(w_names):
                    loaded = sp.dma(raw[:, n, :], ins[w], ch)
                slot, bank, freed = side.take()
                for n in range(4):
                    t = pe.do(lambda e, n=n: e.transpose(bank[:, D * n:D * (n + 1)], raw[:, n, :], ident[:, :]),
                              loaded, freed)
                w_ready = dve.do(lambda e: e.tensor_copy(w_qkv[:, :], bank[:, 0:3 * D]), t)
                w_ready = dve.do(lambda e: e.tensor_copy(w_out[:, :], bank[:, 3 * D:4 * D]), t)
                side.release(slot, w_ready)
                if biases:
                    ch_bias = channel(f"{name}_bias")
                    bias = sb(scope, f"{name}_bias", [4 * D])
                    for n, v in enumerate(biases):
                        b_loaded = sp.dma(bias[:, D * n:D * (n + 1)], ins[v].partition_broadcast(P), ch_bias)
                xn = sb(scope, f"{name}_xn", [TILES, D])
                xnt = sb(scope, f"{name}_xnt", [SEQ])
                qkv = sb(scope, f"{name}_qkv", [TILES, 3 * D])
                turn1 = sb(scope, f"{name}_turn1", [TILES, 2 * D])
                turn2 = y[:, 0:2 * TILES, :].rearrange("p (t s) d -> p t (s d)", t=TILES)
                free = {"xn": None, "xnt": None, "qkv": None, "turn": list(x_loaded)}
                heads = lambda a, lo, hi: a[:, :, lo:hi].rearrange("p t (h d) -> p t h d", d=8)

                def prepare(b, state):
                    xb = x[:, TILES * b:TILES * (b + 1), :]
                    normed = normalise(xb, xn, x_loaded[b], free["xn"])
                    yield
                    parts = transpose_tiles(xn, xnt, side, normed, free["xnt"])
                    free["xn"] = parts[-1]
                    yield
                    for t in range(TILES):
                        slot, bank, freed = side.take()
                        got = pe.do(lambda e: e.matmul(bank[:, 0:3 * D], xnt[:, P * t:P * (t + 1)], w_qkv[:, :],
                                                       start=True, stop=True), parts, w_ready, freed)
                        if biases:
                            end = dve.do(lambda e: e.tensor_tensor(qkv[:, t, :], bank[:, 0:3 * D], bias[:, 0:3 * D],
                                                                   ALU.add), got, b_loaded, free["qkv"])
                        else:
                            end = act.do(lambda e: e.copy(qkv[:, t, :], bank[:, 0:3 * D]), got, free["qkv"])
                        side.release(slot, end)
                        yield
                    free["xnt"] = got
                    for part in range(2):
                        q = heads(qkv, D * part, D * (part + 1))
                        t1 = heads(turn1, D * part, D * (part + 1))
                        t2 = heads(turn2, D * part, D * (part + 1))
                        cos = lambda lo, hi: bcast(small_rot[:, :, rot + lo:rot + hi], 2, 16)
                        pool.do(lambda e: e.tensor_tensor(t1, q, cos(0, 8), ALU.mult), end, free["turn"])
                        yield
                        pool.do(lambda e: e.tensor_tensor(t2[:, :, :, 0:4], q[:, :, :, 4:8], cos(8, 12), ALU.mult))
                        a = pool.do(lambda e: e.tensor_tensor(t2[:, :, :, 4:8], q[:, :, :, 0:4], cos(12, 16), ALU.mult))
                        yield
                        state["rotated"] = pool.do(lambda e: e.tensor_tensor(t1, t1, t2, ALU.add), a)
                        yield
                    state["projected"] = end
                    if biases:
                        state["x"] = pool.do(lambda e: e.tensor_tensor(
                            xb, xb, bcast(bias[:, 3 * D:4 * D], 1, TILES), ALU.add), normed, b_loaded)
                    else:
                        state["x"] = normed
                    yield

                def split(b, state):
                    qslot, qx, qfreed = att.qx.take()
                    state["qx"], state["qslot"] = qx, qslot
                    z = pool.do(lambda e: e.memset(qx[:, :, :, 24:26].bitcast(F32), 0.0), qfreed, att.cleared)
                    rotated = state["rotated"]
                    state["k_split"] = att.split(dve, heads(turn1, D, 2 * D), att.kx, "hlh", rotated,
                                                 [att.cleared, att.kx_free])
                    state["q_split"] = [z, att.split(dve, heads(turn1, 0, D), qx, "hhl", rotated, [att.cleared, qfreed])]
                    free["turn"] = state["q_split"][1]
                    vslot, v, vfreed = att.v.take()
                    state["v"], state["vslot"] = v, vslot
                    state["v_ready"] = dve.do(lambda e: e.tensor_copy(v[:, :, :, 0:8], heads(qkv, 2 * D, 3 * D)),
                                              state["projected"], vfreed, att.cleared)
                    free["qkv"] = [state["v_ready"], rotated]

                def conclude(b, state):
                    parts = transpose_tiles(att.o, xnt2, side, att.o_ready, free.get("xnt2"))
                    att.o_free = parts[-1]
                    yield
                    for c in range(CHUNKS):
                        slot, bank, freed = side.take()
                        for t in range(TPB):
                            got = pe.do(lambda e, t=t: e.matmul(
                                bank[:, P * t:P * (t + 1)], xnt2[:, P * (TPB * c + t):P * (TPB * c + t + 1)],
                                w_out[:, :], start=True, stop=True), parts, freed)
                        rows = x[:, TILES * b + TPB * c:TILES * b + TPB * (c + 1), :]
                        end = dve.do(lambda e: e.tensor_tensor(
                            rows, rows, bank.rearrange("p (t d) -> p t d", t=TPB), ALU.add), got, state["x"])
                        side.release(slot, end)
                        yield
                    free["xnt2"] = got

                xnt2 = sb(scope, f"{name}_xnt2", [SEQ])
                pipeline(att, prepare, split, conclude)
                everyone_waits()

        def local_stage():
            kept = nc.dram_tensor("kept_x", (P, NT, D), F32, kind="Internal").ap()
            with ExitStack() as scope:
                def buf(name, shape, dt=F32):
                    return sb(scope, f"b_{name}", shape, dt)

                proj, turns = Ring(banks[0:2]), Ring(banks[2:4])
                score, out_ring, ff_ring = Ring(banks[4:6]), Ring(banks[6:7]), Ring(banks[7:8])

                ch_small = channel("b_small")
                gain, shift_ = buf("gain", [DEPTH]), buf("shift", [DEPTH])
                b1 = buf("b1", [2, len(FBLOCKS), DEPTH])
                b2 = buf("b2", [DEPTH, D])
                qk_scale = buf("qk_scale", [2, DEPTH, LDIM])
                base_table = buf("base_table", [TILES, 4, LDIM // 2])
                with nc.allow_non_contiguous_dma(reason="parameters by feature, a few thousand words"):
                    sp.dma(gain[:, :], ins["L0_ffn_ln_g"].rearrange("l d -> d l"), ch_small)
                    sp.dma(shift_[:, :], ins["L0_ffn_ln_b"].rearrange("l d -> d l"), ch_small)
                    for part in range(2):
                        for n, (lo, size) in enumerate(FBLOCKS):
                            sp.dma(b1[0:size, part, n, :],
                                   ins["L0_ffn_b1"][:, FF * part + lo:FF * part + lo + size].rearrange("l f -> f l"),
                                   ch_small)
                for n, name in enumerate(("L0_ffn_q_scale", "L0_ffn_k_scale")):
                    sp.dma(qk_scale[:, n, :, :].rearrange("p l d -> p (l d)"),
                           ins[name].rearrange("l d -> (l d)").partition_broadcast(P), ch_small)
                sp.dma(b2[:, :, :].rearrange("p l d -> p (l d)"),
                       ins["L0_ffn_b2"].rearrange("l d -> (l d)").partition_broadcast(P), ch_small)
                small = sp.dma(base_table[:, :, :, :], ins["c_local"].rearrange(
                    "p (t k d) -> p t k d", t=TILES, k=4), ch_small)
                act.wait(small)
                pool.wait(small)

                w_qk = [buf(f"w_qk{n}", [2 * INNER]) for n in range(2)]
                w1, w2 = buf("w1", [2 * FF]), buf("w2", [len(FBLOCKS), D])
                w_v, w_o = buf("w_v", [INNER]), buf("w_o", [PAIRS, D])
                w_vt = w_v[:, :].rearrange("p (a b) -> p a b", a=PAIRS)
                w_vo = [buf(f"w_vo{n}", [4, 4, D]) for n in range(2)]
                table = buf("table", [TILES, 4, LDIM])
                ch_qk, ch_ff = [channel(f"b_qk{n}") for n in range(2)], channel("b_ff")
                ch_vo = channel("b_vo")
                layer = [dict() for _ in range(DEPTH)]
                use = {"qk": [None, None], "ff": None, "vo": [None, None], "raw": None}
                table_ready = [None] * TILES

                def load_layer(l):
                    n, s = l % 2, layer[l]
                    s["qk"] = sp.dma(w_qk[n][:, :], ins["L0_ffn_Wqkv"][l, :, 0:2 * INNER], ch_qk[n], use["qk"][n])
                    sp.dma(w_v[:, :], ins["L0_ffn_Wqkv"][l, :, 2 * INNER:], ch_vo, use["raw"])
                    s["vo_raw"] = sp.dma(w_o[:, :, :], ins["L0_ffn_Wo"][l].rearrange("(c p) d -> p c d", p=P), ch_vo)

                def load_feed_forward(l):
                    full = FF // P
                    sp.dma(w1[:, :], ins["L0_ffn_W1"][l], ch_ff, use["ff"])
                    sp.dma(w2[:, 0:full, :], ins["L0_ffn_W2"][l, 0:full * P, :].rearrange(
                        "(c p) d -> p c d", p=P), ch_ff)
                    layer[l]["ff"] = sp.dma(w2[0:FF - full * P, full, :], ins["L0_ffn_W2"][l, full * P:, :], ch_ff)

                def prepare_table(l, t, free):
                    for k in (0, 2):
                        for half in (slice(0, LDIM // 2), slice(LDIM // 2, LDIM)):
                            table_ready[t] = pool.do(lambda e: e.tensor_tensor(
                                table[:, t, k:k + 2, half], base_table[:, t, k:k + 2, :],
                                bcast(qk_scale[:, k // 2, l, half], 1, 2), ALU.mult), free)

                def prepare_layer(l):
                    n, s = l % 2, layer[l]
                    for c in range(PAIRS // 4):
                        slot, bank, freed = turns.take()
                        for p in range(4):
                            lo = (4 * c + p) * P
                            t = pe.do(lambda e: e.transpose(bank[:, P * p:P * (p + 1)], w_v[:, lo:lo + P], ident[:, :]),
                                      s["vo_raw"], freed, signal=p == 3)
                        turned = dve.do(lambda e: e.tensor_copy(
                            w_vt[:, 4 * c:4 * (c + 1), :].rearrange("p a b -> p (a b)"), bank), t)
                        turns.release(slot, turned)
                        yield
                    for odd in range(2):
                        rows = slice(LDIM * odd, LDIM * (odd + 1))
                        for c in range(PAIRS // 4):
                            slot, bank, freed = turns.take()
                            for p in range(4):
                                t = pe.do(lambda e: e.matmul(
                                    bank[:, D * p:D * (p + 1)], w_vt[rows, 4 * c + p, :], w_o[rows, 4 * c + p, :],
                                    start=True, stop=True), turned, freed, signal=p == 3)
                            got = dve.do(lambda e: e.tensor_copy(
                                w_vo[n][:, odd::2, 2 * c:2 * (c + 1), :].rearrange("p g m d -> p m g d"),
                                bank.rearrange("p (m g d) -> p m g d", m=2, g=2)), t, use["vo"][n])
                            turns.release(slot, got)
                            yield
                    use["raw"], s["vo"] = t, got

                flat = x[:, :, :].rearrange("p t d -> p (t d)")
                part = [flat[:, BANK * n:BANK * (n + 1)] for n in range(8)]
                rot = Ring(part[0:6] + [buf(f"rot{n}", [BANK])[:, :] for n in range(2)])
                square = Ring(part[6:8])
                cross = Ring([buf(f"cross{n}", [BANK]) for n in range(3)])
                norm = Ring([buf(f"norm{n}", [3, 2 * LHEADS]) for n in range(2)])
                xs = Ring([buf(f"xs{n}", [TILES, D]) for n in range(2)])
                xst = Ring([buf(f"xst{n}", [SEQ]) for n in range(2)])
                xnt = Ring([buf("xnt", [SEQ])])
                q_t = Ring([buf(f"q_t{n}", [PAIRS, P]) for n in range(2)])
                k_t = buf("k_t", [PAIRS, 2, 3, P])
                v_w = buf("v_w", [3 * WPT, 4, D])
                k_ring, v_ring = Ring([0, 1, 2]), Ring([0, 1, 2])
                prob = Ring([buf(f"prob{n}", [2, HPC, WINDOW]) for n in range(4)])
                prob_t = Ring([buf(f"prob_t{n}", [4, P]) for n in range(3)])
                stat = Ring([buf(f"stat{n}", [3, HPC]) for n in range(4)])
                hidden = Ring([buf(f"hidden{n}", [len(FBLOCKS), BANK]) for n in range(1)])
                ch_xs = [channel(f"b_xs{n}") for n in range(2)]
                z = [pool.do(lambda e: e.memset(t[:], 0.0)) for t in [k_t] + hidden.views]
                act.wait(z[-1])
                dve.wait(z[-1])

                y_ready = [None] * BATCH

                def shifted(b):
                    slot, buffer, freed = xs.take()
                    t0, half, ch = TILES * b, D // 2, ch_xs[slot]
                    rows = y[:, t0:t0 + TILES, :]
                    z = pool.do(lambda e: e.memset(buffer[0:1, 0, half:D], 0.0), freed)
                    sp.dma(buffer[:, :, 0:half], rows[:, :, 0:half], ch, y_ready[b], freed, z)
                    sp.dma(buffer[1:P, :, half:D], rows[0:P - 1, :, half:D], ch)
                    moved = sp.dma(buffer[0:1, 1:TILES, half:D], rows[P - 1:P, 0:TILES - 1, half:D], ch)
                    return slot, buffer, [moved, z]

                batches, fed_forward = {}, set()

                def open_batch(l, b):
                    assert l == 0 or (l - 1, b) in fed_forward
                    slot, buffer, loaded = shifted(b)
                    yield
                    yield
                    tslot, turned, freed = xst.take()
                    ready = transpose_tiles(buffer, turned, turns, loaded, freed)
                    xs.release(slot, ready)
                    batches[l, b] = {"xst": turned, "slot": tslot, "ready": ready}
                    yield

                tiles = {}

                def project(l, b, t):
                    s, info = batches[l, b], {"rot": []}
                    tiles[l, b, t] = info
                    nslot, nm, nfreed = norm.take()
                    for c in range(4):
                        slot, bank, freed = proj.take()
                        got = pe.do(lambda e: e.matmul(bank, s["xst"][:, P * t:P * (t + 1)],
                                                       w_qk[l % 2][:, BANK * c:BANK * (c + 1)], start=True, stop=True),
                                    s["ready"], layer[l]["qk"], freed)
                        heads = bank.rearrange("p (h d) -> p h d", h=HPC)
                        sslot, sq, sfreed = square.take()
                        squared = act.do(lambda e: e.activation(sq, bank, ACT.Square), got, sfreed)
                        yield
                        rslot, r, rfreed = rot.take()
                        cslot, x2, cfreed = cross.take()
                        k = 2 * (c // 2)
                        rh, xh = (a.rearrange("p (h d) -> p h d", h=HPC) for a in (r, x2[:, :]))
                        straight = dve.do(lambda e: e.tensor_tensor(
                            rh, heads, bcast(table[:, t, k, :], 1, HPC), ALU.mult), squared, rfreed, table_ready[t])
                        crossed = dve.do(lambda e: e.tensor_tensor(
                            xh, heads, bcast(table[:, t, k + 1, :], 1, HPC), ALU.mult), cfreed)
                        proj.release(slot, crossed)
                        summed = dve.do(lambda e: e.tensor_reduce(
                            nm[:, 0, HPC * c:HPC * (c + 1)], sq.rearrange("p (h d) -> p h d", h=HPC), AX.X, ALU.add),
                            squared, nfreed)
                        square.release(sslot, summed)
                        half = LDIM // 2
                        for a, o, op in ((0, half, ALU.subtract), (half, 0, ALU.add)):
                            added = pool.do(lambda e: e.tensor_tensor(
                                rh[:, :, a:a + half], rh[:, :, a:a + half], xh[:, :, o:o + half], op), crossed)
                        cross.release(cslot, added)
                        info["rot"].append((rslot, r, added))
                        yield
                    use["qk"][l % 2] = got
                    if b == BATCH - 1 and l + 1 < DEPTH:
                        prepare_table(l + 1, t, crossed)
                    held = dve.do(lambda e: e.tensor_scalar(nm[:, 0, :], nm[:, 0, :], 1e-24, None, ALU.max), summed)
                    inv = inverse_root(dve, nm[:, 1, :], nm[:, 0, :], nm[:, 2, :], held)
                    for c, (rslot, r, added) in enumerate(info["rot"]):
                        rh = r.rearrange("p (h d) -> p h d", h=HPC)
                        scaled = pool.do(lambda e: e.tensor_tensor(
                            rh, rh, bcast(nm[:, 1, HPC * c:HPC * (c + 1)], 2, LDIM), ALU.mult), inv, added)
                        info["rot"][c] = (rslot, r, scaled)
                        yield
                    norm.release(nslot, scaled)

                def turn(l, b, t):
                    s, info = batches[l, b], tiles[l, b, t]
                    qslot, qt, qfreed = q_t.take()
                    kslot, _, kfreed = k_ring.take()
                    vslot, _, vfreed = v_ring.take()
                    for c in range(4):
                        rslot, r, scaled = info["rot"][c]
                        slot, bank, freed = turns.take()
                        for p in range(4):
                            turned = pe.do(lambda e: e.transpose(bank[:, P * p:P * (p + 1)], r[:, P * p:P * (p + 1)],
                                                                 ident[:, :]), scaled, freed, signal=p == 3)
                        rot.release(rslot, turned)
                        pairs = slice(4 * (c % 2), 4 * (c % 2) + 4)
                        by_pair = bank.rearrange("p (a q) -> p a q", a=4)
                        if c < 2:
                            got = act.do(lambda e: e.copy(qt[:, pairs, :], by_pair), turned, qfreed)
                            turns.release(slot, got)
                            info["q"] = got
                        else:
                            lo = act.do(lambda e: e.copy(k_t[0:LDIM, pairs, 0, kslot, :], by_pair[0:LDIM]),
                                        turned, kfreed)
                            hi = act.do(lambda e: e.copy(k_t[LDIM:P, pairs, 1, kslot, :], by_pair[LDIM:P]),
                                        turned, kfreed)
                            turns.release(slot, lo, hi)
                            info["k"] = [lo, hi]
                        yield
                        w = c
                        slot, bank, freed = proj.take()
                        for g in range(4):
                            got = pe.do(lambda e: e.matmul(
                                bank[WINDOW * g:WINDOW * (g + 1), :],
                                s["xst"][:, P * t + WINDOW * w:P * t + WINDOW * (w + 1)],
                                w_vo[l % 2][:, g, :, :].rearrange("p m d -> p (m d)"), start=True, stop=True,
                                tile_position=(0, WINDOW * g)), layer[l]["vo"], freed, signal=g == 3)
                        v = v_w[:, WPT * vslot + w, :, :].rearrange("p m d -> p (m d)")
                        info["v"] = act.do(lambda e: e.copy(v, bank), got, vfreed)
                        proj.release(slot, info["v"])
                        yield
                    use["vo"][l % 2] = got
                    info.update(qslot=qslot, qt=qt, kslot=kslot, vslot=vslot)
                    if t == TILES - 1:
                        xst.release(s["slot"], got)

                def per_head(ap):
                    return bcast(bcast(ap, 1, 2), 3, WINDOW)

                def attend(l, b, t):
                    info = tiles[l, b, t]
                    before = tiles[l, b, t - 1] if t else None
                    mask = opening_mask if t == 0 else window_mask
                    ks, qt = info["kslot"], info["qt"]
                    info["prob"] = []
                    for c in range(2):
                        slot, bank, freed = score.take()
                        halves = bank.rearrange("p (s h k) -> p s h k", s=2, h=HPC)
                        pe.do(lambda e: e.matmul(
                            halves, ident_bf[:, :], bcast(mask.rearrange("p (s k) -> p s k", s=2), 2, HPC),
                            start=True, stop=False, skip_group_check=True),
                              freed, info["q"], info["k"], before and before["k"], signal=False)
                        by_head = bank.rearrange("p (s h k) -> p h s k", s=2, h=HPC)
                        for p in range(4):
                            for w in range(WPT):
                                q = qt[:, 4 * c + p, WINDOW * w:WINDOW * (w + 1)]
                                rows = slice(WINDOW * w, WINDOW * (w + 1))
                                k = k_t[:, 4 * c + p, :, :, :].rearrange("p h s q -> p h (s q)")
                                at = P * ks + WINDOW * (w - 1)
                                if w or (t and ks):
                                    spans = [(at, slice(0, 2))]
                                else:
                                    spans = [(at + WINDOW, slice(1, 2))]
                                    if t:
                                        spans.append((P * 3 - WINDOW, slice(0, 1)))
                                for lo, to in spans:
                                    n = WINDOW * (to.stop - to.start)
                                    got = pe.do(lambda e: e.matmul(
                                        by_head[rows, 2 * p:2 * p + 2, to, :], q, k[:, :, lo:lo + n].rearrange(
                                            "p h (s q) -> p h s q", q=WINDOW),
                                        start=False, stop=True, skip_group_check=True,
                                        tile_position=(0, WINDOW * w)), signal=p == 3 and w == WPT - 1)
                            if p == 1:
                                yield
                        sslot, st, sfreed = stat.take()
                        pslot, pr, pfreed = prob.take()
                        top = dve.do(lambda e: e.tensor_reduce(st[:, 0, :], by_head, AX.XY, ALU.max), got, sfreed)
                        less = dve.do(lambda e: e.tensor_tensor(
                            pr[:, :, :, :], halves, per_head(st[:, 0, :]), ALU.subtract), top, pfreed)
                        score.release(slot, less)
                        yield
                        power = act.do(lambda e: e.activation(pr[:, :, :, :], pr[:, :, :, :], ACT.Exp), less)
                        yield
                        total = dve.do(lambda e: e.tensor_reduce(
                            st[:, 1, :], pr[:, :, :, :].rearrange("p s h k -> p h s k"), AX.XY, ALU.add), power)
                        inv = dve.do(lambda e: e.reciprocal(st[:, 2, :], st[:, 1, :]), total)
                        done = pool.do(lambda e: e.tensor_tensor(
                            pr[:, :, :, :], pr[:, :, :, :], per_head(st[:, 2, :]), ALU.mult), inv)
                        stat.release(sslot, done)
                        info["prob"].append((pslot, pr, done))
                        yield
                    q_t.release(info["qslot"], got)
                    if before:
                        k_ring.release(before["kslot"], got)
                    if t == TILES - 1:
                        k_ring.release(ks, got)

                def combine(l, b, t):
                    info = tiles[l, b, t]
                    before = tiles[l, b, t - 1] if t else None
                    oslot, obank, ofreed = out_ring.take()
                    started = set()
                    for c in range(2):
                        pslot, pr, ready = info["prob"][c]
                        slot, bank, freed = turns.take()
                        for j in range(4):
                            m, half = j // 2, j % 2
                            turned = pe.do(lambda e: e.transpose(
                                bank[:, P * j:P * (j + 1)],
                                pr[:, half, 4 * m:4 * (m + 1), :].rearrange("p g k -> p (g k)"), ident[:, :]),
                                ready, freed, signal=j == 3)
                        prob.release(pslot, turned)
                        tslot, pt, tfreed = prob_t.take()
                        got = act.do(lambda e: e.copy(pt[:, :, :].rearrange("p j q -> p (j q)"), bank), turned, tfreed)
                        turns.release(slot, got)
                        yield
                        for j in range(4):
                            m, half = 2 * c + j // 2, j % 2
                            for w in range(WPT):
                                if half == 0 and w == 0:
                                    if not t:
                                        continue
                                    at = WPT * before["vslot"] + WPT - 1
                                else:
                                    at = WPT * info["vslot"] + w - 1 + half
                                rows = slice(WINDOW * w, WINDOW * (w + 1))
                                done = pe.do(lambda e: e.matmul(
                                    obank[rows, 0:D], pt[:, j, rows], v_w[:, at, m, :], start=w not in started,
                                    stop=c == 1 and j == 3, skip_group_check=True, tile_position=(0, WINDOW * w)),
                                    got, info["v"], before and before["v"], ofreed, signal=j == 3 and w == WPT - 1)
                                started.add(w)
                        prob_t.release(tslot, done)
                        yield
                    rows = y[:, TILES * b + t, :]
                    end = dve.do(lambda e: e.tensor_tensor(rows, rows, obank[:, 0:D], ALU.add), done, y_ready[b])
                    out_ring.release(oslot, end)
                    info["y"] = end
                    if before:
                        v_ring.release(before["vslot"], done)
                    if t == TILES - 1:
                        v_ring.release(info["vslot"], done)
                        y_ready[b] = [end]

                def feed_forward(l, b):
                    s = layer[l]
                    slot, buffer, loaded = shifted(b)
                    yield
                    rows = y[:, TILES * b:TILES * (b + 1), :]
                    biased = pool.do(lambda e: e.tensor_tensor(rows, rows, bcast(b2[:, l, :], 1, TILES), ALU.add),
                                     loaded, y_ready[b])
                    yield
                    yield
                    normed = normalise(buffer, buffer, loaded, None)
                    yield
                    xslot, xn, xfreed = xnt.take()
                    ready = transpose_tiles(buffer, xn, ff_ring, normed, xfreed, evacuate=lambda e, o, i: e.activation(
                        o, i, ACT.Identity, bias=shift_[:, l:l + 1], scale=gain[:, l:l + 1]))
                    xs.release(slot, ready)
                    yield
                    for c in range(CHUNKS):
                        hslot, hid, hfreed = hidden.take()
                        for part in (1, 0):
                            for f, (lo, size) in enumerate(FBLOCKS):
                                bslot, bank, freed = ff_ring.take()
                                got = pe.do(lambda e: e.matmul(
                                    bank[0:size, :], w1[:, FF * part + lo:FF * part + lo + size],
                                    xn[:, BANK * c:BANK * (c + 1)], start=True, stop=True), ready, s["ff"], freed)
                                bias = b1[0:size, part, f, l:l + 1]
                                if part:
                                    moved = act.do(lambda e: e.activation(
                                        hid[0:size, f, :], bank[0:size, :], ACT.Identity, bias=bias), got, hfreed)
                                    ff_ring.release(bslot, moved)
                                else:
                                    made = dve.do(lambda e: e.scalar_tensor_tensor(
                                        out=hid[0:size, f, :], in0=bank[0:size, :], scalar=bias,
                                        in1=hid[0:size, f, :], op0=ALU.add, op1=ALU.mult), got, opened)
                                    ff_ring.release(bslot, made)
                                yield
                            if part:
                                opened = act.do(lambda e: e.activation(hid[:], hid[:], ACT.Gelu), moved)
                                yield
                        bslot, bank, freed = ff_ring.take()
                        for t in range(TPB):
                            for f, (lo, size) in enumerate(FBLOCKS):
                                got = pe.do(lambda e: e.matmul(
                                    bank[:, P * t:P * (t + 1)], hid[0:size, f, P * t:P * (t + 1)], w2[0:size, f, :],
                                    start=f == 0, stop=f == len(FBLOCKS) - 1), made, freed,
                                    signal=t == TPB - 1 and f == len(FBLOCKS) - 1)
                            yield
                        hidden.release(hslot, got)
                        part = rows[:, TPB * c:TPB * (c + 1), :]
                        end = dve.do(lambda e: e.tensor_tensor(
                            part, part, bank.rearrange("p (t d) -> p t d", t=TPB), ALU.add), got, biased)
                        ff_ring.release(bslot, end)
                        yield
                    xnt.release(xslot, got)
                    use["ff"] = got
                    y_ready[b] = [end]
                    fed_forward.add((l, b))

                stream = [(l, b, t) for l in range(DEPTH) for b in range(BATCH) for t in range(TILES)]
                load_layer(0)
                for t in range(TILES):
                    prepare_table(0, t, None)
                for b in range(BATCH):
                    batch = slice(TILES * b, TILES * (b + 1))
                    y_ready[b] = [normalise(x[:, batch, :], y[:, batch, :], x_loaded[b], None)]
                    if b == 0:
                        run(open_batch(0, 0))
                x_kept = sp.dma(kept, x[:, :, :], channel("b_kept"), x_loaded)
                run(prepare_layer(0))
                for e in (dve, act, pool):
                    e.wait(x_kept, y_ready[-1])
                opening, preparing, fed, active = [], [], [], []
                last_start = ROUNDS * (len(stream) - 1) + max(LAGS)
                now = 0
                while now <= last_start or active:
                    for lag, stage in zip(LAGS, (project, turn, attend, combine)):
                        i, rest = divmod(now - lag, ROUNDS)
                        if rest or not 0 <= i < len(stream):
                            continue
                        l, b, t = stream[i]
                        active.append((i, stage(l, b, t)))
                        if stage is project:
                            if b == 0 and t == 3 and l + 1 < DEPTH:
                                load_layer(l + 1)
                            if b == 1 and t == 2:
                                load_feed_forward(l)
                            if b == 1 and t == 3 and l + 1 < DEPTH:
                                preparing.append(prepare_layer(l + 1))
                            if t == TILES - 2 and i + 2 < len(stream):
                                opening.append(open_batch(*stream[i + 2][0:2]))
                    active.sort(key=lambda w: w[0])
                    still = []
                    for i, work in active:
                        if next(work, active) is not active:
                            still.append((i, work))
                        elif "y" in tiles[stream[i]] and stream[i][2] == TILES - 1 and not tiles[stream[i]].get("fed"):
                            tiles[stream[i]]["fed"] = True
                            fed.append(feed_forward(*stream[i][0:2]))
                    active = still
                    for queue, (every, at) in ((opening, OPENING_EVERY), (fed, FED_EVERY),
                                               (preparing, PREPARING_EVERY)):
                        if queue and now % every == at and next(queue[0], active) is active:
                            queue.pop(0)
                    now += 1
                run(chain(*fed))

                everyone_waits()
                for b in range(BATCH):
                    rows = slice(TILES * b, TILES * (b + 1))
                    back = sp.dma(x[:, rows, :], kept[:, rows, :], ch_x[b])
                    x_loaded[b] = (dve, pool)[b % 2].do(lambda e: e.tensor_tensor(
                        x[:, rows, :], x[:, rows, :], y[:, rows, :], ALU.add), back)

        def moe_stage():
            with ExitStack() as kept:
                experts = load_experts(kept)
                moe_attention(experts)
                moe_experts(experts)

        def load_experts(kept):
            ch = channel("d_experts")
            n_w = EXPERTS + 1
            raw = [sb(kept, f"d_raw{k}", [n_w, D]) for k in range(3)]
            turned = [sb(kept, f"d_turned{k}", [n_w, D]) for k in range(3)]
            for k, (own, shared) in enumerate((("L1_ffn_eW1", "L1_ffn_sW1"), ("L1_ffn_eW3", "L1_ffn_sW3"),
                                               ("L1_ffn_eW2", "L1_ffn_sW2"))):
                sp.dma(raw[k][:, 0:EXPERTS, :], ins[own].rearrange("e a b -> a e b"), ch)
                sp.dma(raw[k][:, EXPERTS, :], ins[shared], ch)
            router_raw = sb(kept, "d_router_raw", [D])
            router = sb(kept, "d_router", [EXPERTS])
            bias = sb(kept, "d_bias", [EXPERTS])
            gains2 = sb(kept, "d_gains2", [1])
            numbers = sb(kept, "d_numbers", [EXPERTS])
            sp.dma(router_raw[0:EXPERTS, :], ins["L1_ffn_Wr"], ch)
            sp.dma(bias[:, :], ins["L1_ffn_expert_bias"].partition_broadcast(P), ch)
            sp.dma(numbers[:, :], ins["c_masks"][:, CONST_WIDTH - EXPERTS:CONST_WIDTH], ch)
            experts_loaded = sp.dma(gains2[:, :], ins["L1_ffn_g2"].rearrange("(d o) -> d o", o=1), ch)
            return dict(raw=raw, turned=turned, router_raw=router_raw, router=router, bias=bias, gains=gains2,
                        numbers=numbers, loaded=experts_loaded)

        def moe_attention(experts):
            with ExitStack() as scope:
                att = FullAttention(scope, "d", DDIM, False, float(1.0 / np.sqrt(np.float32(DDIM))), False)
                side, qkv_width = att.side, D + 2 * DDIM
                ch = channel("d_w")
                raw = sb(scope, "d_raw", [2, D])
                small_raw = sb(scope, "d_small_raw", [2 * D])
                w_qkv, w_out = sb(scope, "d_w_qkv", [qkv_width]), sb(scope, "d_w_out", [D])
                gains = sb(scope, "d_gains", [1])
                sp.dma(raw[:, 0, :], ins["L1_ffn_Wq"], ch)
                sp.dma(raw[:, 1, :], ins["L1_ffn_Wo"], ch)
                sp.dma(small_raw[0:DDIM, 0:D], ins["L1_ffn_Wkc"], ch)
                sp.dma(small_raw[0:DDIM, D:2 * D], ins["L1_ffn_Wvc"], ch)
                loaded = sp.dma(gains[:, :], ins["L1_ffn_g1"].rearrange("(d o) -> d o", o=1), ch)
                act.wait(loaded)
                slot, bank, freed = side.take()
                pe.do(lambda e: e.transpose(bank[:, 0:D], raw[:, 0, :], ident[:, :]), loaded, freed, signal=False)
                for n in range(2):
                    pe.do(lambda e: e.transpose(bank[:, D + DDIM * n:D + DDIM * (n + 1)],
                                                small_raw[0:DDIM, D * n:D * (n + 1)], ident[0:DDIM, 0:DDIM]),
                          signal=False)
                t = pe.do(lambda e: e.transpose(bank[:, qkv_width:qkv_width + D], raw[:, 1, :], ident[:, :]))
                dve.do(lambda e: e.tensor_copy(w_qkv[:, :], bank[:, 0:qkv_width]), t)
                w_ready = dve.do(lambda e: e.tensor_copy(w_out[:, :], bank[:, qkv_width:qkv_width + D]), t)
                side.release(slot, w_ready)
                raw, turned, router_raw, router = (experts[k] for k in ("raw", "turned", "router_raw", "router"))
                n_w, experts_loaded = EXPERTS + 1, experts["loaded"]
                slot, bank, freed = side.take()
                t = pe.do(lambda e: e.transpose(bank[:, 0:EXPERTS], router_raw[0:EXPERTS, :],
                                                ident[0:EXPERTS, 0:EXPERTS]), experts_loaded, freed)
                experts_ready = act.do(lambda e: e.copy(router[:, :], bank[:, 0:EXPERTS]), t)
                side.release(slot, experts_ready)
                for k in range(3):
                    for lo in range(0, n_w, 4):
                        hi = min(n_w, lo + 4)
                        slot, bank, freed = side.take()
                        for n in range(lo, hi):
                            t = pe.do(lambda e: e.transpose(bank[:, D * (n - lo):D * (n - lo + 1)], raw[k][:, n, :],
                                                            ident[:, :]), freed, signal=n == hi - 1)
                        experts_ready = act.do(lambda e: e.copy(
                            turned[k][:, lo:hi, :].rearrange("p a b -> p (a b)"), bank[:, 0:D * (hi - lo)]), t)
                        side.release(slot, experts_ready)
                experts["ready"] = experts_ready
                yn = sb(scope, "d_yn", [TILES, D])
                ynt = sb(scope, "d_ynt", [SEQ])
                qkv = sb(scope, "d_qkv", [TILES, qkv_width])
                free = {}

                def prepare(b, state):
                    tiles = slice(TILES * b, TILES * (b + 1))
                    inner = yield from normalise_steps(x[:, tiles, :], y[:, tiles, :], x_loaded[b], None)
                    yield
                    normed = yield from normalise_steps(y[:, tiles, :], yn, inner, free.get("yn"), rms=True)
                    yield
                    parts = transpose_tiles(yn, ynt, side, normed, free.get("ynt"), evacuate=lambda e, o, i: e.activation(
                        o, i, ACT.Identity, scale=gains[:, 0:1]))
                    free["yn"] = parts[-1]
                    yield
                    for t in range(TILES):
                        slot, bank, freed = side.take()
                        got = pe.do(lambda e: e.matmul(bank[:, 0:qkv_width], ynt[:, P * t:P * (t + 1)], w_qkv[:, :],
                                                       start=True, stop=True), parts, w_ready, freed)
                        end = dve.do(lambda e: e.tensor_copy(qkv[:, t, :], bank[:, 0:qkv_width]), got, free.get("qkv"))
                        side.release(slot, end)
                        yield
                    free["ynt"] = got
                    state["projected"] = end

                def split(b, state):
                    heads = lambda lo, n: qkv[:, :, lo:lo + n * DDIM].rearrange(
                        "p t (h d) -> p t h d", d=DDIM)
                    end = state["projected"]
                    qslot, qx, qfreed = att.qx.take()
                    state["qx"], state["qslot"] = qx, qslot
                    z = pool.do(lambda e: e.memset(qx[:, :, :, 3 * DDIM:3 * DDIM + 2].bitcast(F32), 0.0),
                                qfreed, att.cleared)
                    state["k_split"] = att.split(dve, heads(D, 1), att.kx, "hlh", end, [att.cleared, att.kx_free])
                    state["q_split"] = [z, att.split(dve, heads(0, DHEADS), qx, "hhl", end, [att.cleared, qfreed])]
                    vslot, v, vfreed = att.v.take()
                    state["v"], state["vslot"] = v, vslot
                    state["v_ready"] = dve.do(lambda e: e.tensor_copy(v[:, :, :, 0:DDIM], heads(D + DDIM, 1)),
                                              end, vfreed, att.cleared)
                    free["qkv"] = state["v_ready"]

                def conclude(b, state):
                    for c in range(CHUNKS):
                        slot, bank, freed = side.take()
                        for t in range(TPB):
                            got = pe.do(lambda e: e.matmul(
                                bank[:, P * t:P * (t + 1)], att.ot[:, P * (TPB * c + t):P * (TPB * c + t + 1)],
                                w_out[:, :], start=True, stop=True), att.ot_ready, freed, signal=t == TPB - 1)
                        rows = y[:, TILES * b + TPB * c:TILES * b + TPB * (c + 1), :]
                        end = dve.do(lambda e: e.tensor_tensor(
                            rows, rows, bank.rearrange("p (t d) -> p t d", t=TPB), ALU.add), got)
                        side.release(slot, end)
                        yield
                    att.ot_free = got

                pipeline(att, prepare, split, conclude)
                everyone_waits()

        def moe_experts(experts):
            with ExitStack() as scope:
                turned, router, bias, gains, numbers = (experts[k] for k in ("turned", "router", "bias", "gains", "numbers"))
                w_ready, n_w = experts["ready"], EXPERTS + 1
                hidden_ring, out_ring, misc = Ring(banks[0:4]), Ring(banks[4:6]), Ring(banks[6:8])
                w1t, w3t, w2t = turned
                yn = Ring([sb(scope, f"d_yn{n}", [TILES, D]) for n in range(2)])
                ynt = Ring([sb(scope, f"d_ynt{n}", [SEQ]) for n in range(2)])
                gate = Ring([sb(scope, f"d_gate{n}", [BANK]) for n in range(2)])
                hid = Ring([sb(scope, f"d_hid{n}", [BANK]) for n in range(2)])
                part = Ring([sb(scope, f"d_part{n}", [BANK]) for n in range(2)])
                te = lambda name, n=EXPERTS, dt=F32: sb(scope, f"d_{name}", [TILES, n], dt)
                logits, weights, best, chosen = te("logits"), te("weights"), te("best"), te("chosen")
                where = te("where", EXPERTS, U32)
                second, combine = te("second"), Ring([te(f"combine{n}") for n in range(2)])
                one = sb(scope, "d_one", [5, TILES])
                act.wait(experts["loaded"])
                routed, share_out = [None], {}

                def route(b):
                    rows = y[:, TILES * b:TILES * (b + 1), :]
                    nslot, yb, nfreed = yn.take()
                    normed = yield from normalise_steps(rows, yb, None, nfreed, rms=True)
                    yield
                    tslot, yt, tfreed = ynt.take()
                    ready = transpose_tiles(yb, yt, misc, normed, tfreed, evacuate=lambda e, o, i: e.activation(
                        o, i, ACT.Identity, scale=gains[:, 0:1]))
                    yn.release(nslot, ready)
                    yield
                    slot, bank, freed = misc.take()
                    for t in range(TILES):
                        got = pe.do(lambda e: e.matmul(bank[:, EXPERTS * t:EXPERTS * (t + 1)], yt[:, P * t:P * (t + 1)],
                                                       router[:, :], start=True, stop=True),
                                    ready, w_ready, freed, signal=t == TILES - 1)
                    scores = bank[:, 0:EXPERTS * TILES].rearrange("p (t e) -> p t e", t=TILES)
                    across = lambda ap: bcast(ap, 2, EXPERTS)
                    a = dve.do(lambda e: e.tensor_tensor(logits[:], scores, bcast(bias[:, :], 1, TILES), ALU.add),
                               got, routed[0])
                    misc.release(slot, a)
                    yield
                    a = dve.do(lambda e: e.tensor_reduce(one[:, 0, :], logits[:], AX.X, ALU.max), a)
                    a = dve.do(lambda e: e.tensor_tensor(logits[:], logits[:], across(one[:, 0, :]), ALU.subtract), a)
                    a = act.do(lambda e: e.activation(weights[:], logits[:], ACT.Exp), a)
                    yield
                    a = dve.do(lambda e: e.tensor_reduce(one[:, 1, :], weights[:], AX.X, ALU.add), a)
                    a = dve.do(lambda e: e.reciprocal(one[:, 2, :], one[:, 1, :]), a)
                    a = dve.do(lambda e: e.tensor_tensor(weights[:], weights[:], across(one[:, 2, :]), ALU.mult), a)
                    for t in range(TILES):
                        m = dve.do(lambda e: e.max(best[:, t, :], weights[:, t, :]), a)
                    yield
                    for t in range(TILES):
                        n = dve.do(lambda e: e.max_index(where[:, t, :], best[:, t, :], weights[:, t, :]), m)
                    n = dve.do(lambda e: e.tensor_copy(chosen[:], where[:]), n)
                    yield
                    a = dve.do(lambda e: e.tensor_tensor(one[:, 3, :], best[:, :, 1], best[:, :, 0], ALU.subtract), m)
                    a = act.do(lambda e: e.activation(one[:, 4, :], one[:, 3, :], ACT.Exp), a)
                    yield
                    a = dve.do(lambda e: e.tensor_scalar(one[:, 3, :], one[:, 4, :], 1.0, None, ALU.add), a)
                    a = dve.do(lambda e: e.reciprocal(one[:, 2, :], one[:, 3, :]), a)
                    a = dve.do(lambda e: e.tensor_tensor(one[:, 1, :], one[:, 4, :], one[:, 2, :], ALU.mult), a)
                    cslot, share, cfreed = combine.take()
                    each = bcast(numbers[:, :], 1, TILES)
                    f = dve.do(lambda e: e.tensor_tensor(share[:], each, across(chosen[:, :, 0]), ALU.is_equal),
                               n, cfreed)
                    g = dve.do(lambda e: e.tensor_tensor(second[:], each, across(chosen[:, :, 1]), ALU.is_equal), n)
                    f = dve.do(lambda e: e.tensor_tensor(share[:], share[:], across(one[:, 2, :]), ALU.mult), f, a)
                    g = dve.do(lambda e: e.tensor_tensor(second[:], second[:], across(one[:, 1, :]), ALU.mult), g, a)
                    routed[0] = dve.do(lambda e: e.tensor_tensor(share[:], share[:], second[:], ALU.add), f, g)
                    share_out[b] = (normed, ready, tslot, yt, cslot, share, routed[0])

                def up(b, x_no, c):
                    _, ready, _, yt, *_ = share_out[b]
                    cols = slice(BANK * c, BANK * (c + 1))
                    s1, bank1, f1 = hidden_ring.take()
                    s3, bank3, f3 = hidden_ring.take()
                    g1 = pe.do(lambda e: e.matmul(bank1, w1t[:, x_no, :], yt[:, cols], start=True, stop=True),
                               ready, w_ready, f1)
                    g3 = pe.do(lambda e: e.matmul(bank3, w3t[:, x_no, :], yt[:, cols], start=True, stop=True), f3)
                    gs, gt, gf = gate.take()
                    opened = act.do(lambda e: e.activation(gt[:, :], bank1, ACT.Silu), g1, gf)
                    hidden_ring.release(s1, opened)
                    hs, ht, hf = hid.take()
                    made = dve.do(lambda e: e.tensor_tensor(ht[:, :], gt[:, :], bank3, ALU.mult), g3, opened, hf)
                    hidden_ring.release(s3, made)
                    gate.release(gs, made)
                    return hs, ht, made

                def down(b, x_no, c, hs, ht, made):
                    rows = y[:, TILES * b:TILES * (b + 1), :]
                    _, _, tslot, _, cslot, share, chosen_ready = share_out[b]
                    os, bank, of = out_ring.take()
                    for t in range(TPB):
                        got = pe.do(lambda e: e.matmul(bank[:, D * t:D * (t + 1)], ht[:, P * t:P * (t + 1)],
                                                       w2t[:, x_no, :], start=True, stop=True),
                                    made, of, signal=t == TPB - 1)
                    hid.release(hs, got)
                    by_tile = bank.rearrange("p (t d) -> p t d", t=TPB)
                    tiles = slice(TPB * c, TPB * (c + 1))
                    if x_no < EXPERTS:
                        ps, pt, pf = part.take()
                        pt = pt[:, :].rearrange("p (t d) -> p t d", t=TPB)
                        scaled = dve.do(lambda e: e.tensor_tensor(
                            pt, by_tile, bcast(share[:, tiles, x_no], 2, D), ALU.mult), got, chosen_ready, pf)
                        out_ring.release(os, scaled)
                        summed[b, c] = pool.do(lambda e: e.tensor_tensor(
                            rows[:, tiles, :], rows[:, tiles, :], pt, ALU.add), scaled, summed[b, c])
                        part.release(ps, summed[b, c])
                        if (x_no, c) == (EXPERTS - 1, CHUNKS - 1):
                            combine.release(cslot, scaled)
                        return
                    summed[b, c] = dve.do(lambda e: e.tensor_tensor(
                        rows[:, tiles, :], rows[:, tiles, :], by_tile, ALU.add), got, summed[b, c])
                    out_ring.release(os, summed[b, c])
                    if c == CHUNKS - 1:
                        batch = slice(TILES * b, TILES * (b + 1))
                        x_loaded[b] = pool.do(lambda e: e.tensor_tensor(
                            x[:, batch, :], x[:, batch, :], y[:, batch, :], ALU.add),
                            [summed[b, k] for k in range(CHUNKS)])

                summed = {}
                run(route(0))
                waiting = None
                for b in range(BATCH):
                    for c in range(CHUNKS):
                        summed[b, c] = share_out[b][0]
                    coming = route(b + 1) if b + 1 < BATCH else iter(())
                    for n, (x_no, c) in enumerate((e, c) for e in range(n_w) for c in range(CHUNKS)):
                        made = up(b, x_no, c)
                        if (x_no, c) == (n_w - 1, CHUNKS - 1):
                            ynt.release(share_out[b][2], pe.last())
                        if waiting:
                            down(*waiting)
                        waiting = (b, x_no, c, *made)
                        next(coming, None)
                    run(coming)
                down(*waiting)

        if "A" in stages:
            mha_stage("a", ("L0_attn_wq", "L0_attn_wk", "L0_attn_wv", "L0_attn_wo"),
                      ("L0_attn_bq", "L0_attn_bk", "L0_attn_bv", "L0_attn_bo"), 0, False)
        if "B" in stages:
            local_stage()
        if "C" in stages:
            mha_stage("c", ("L1_attn_W_Q", "L1_attn_W_K", "L1_attn_W_V", "L1_attn_W_O"), (), 16, True)

        if "D" in stages:
            moe_stage()

        ch_out = channel("out")
        stored = sp.dma(out.rearrange("b (t p) d -> p (b t) d", p=P), x[:, :, :], ch_out,
                        dve.last(), pool.last(), act.last())
        sp.wait(stored)


def kernel(**inputs):
    import concourse.bacc as bacc
    from concourse.bass_utils import run_bass_kernel_spmd

    nc = bacc.Bacc("TRN2", target_bir_lowering=False, num_devices=1)
    small, local = rotary_constants()
    given = {name: np.ascontiguousarray(value) for name, value in inputs.items()}
    given.update(c_small=small, c_local=local, c_masks=mask_constants())
    arrays = {f"in_{name}": value for name, value in given.items()}
    ins = {name: nc.dram_tensor(f"in_{name}", value.shape, mybir.dt.from_np(value.dtype),
                                kind="ExternalInput").ap() for name, value in given.items()}
    out = nc.dram_tensor("out_x", (BATCH, SEQ, D), F32, kind="ExternalOutput").ap()
    build(nc, ins, out)
    return run_bass_kernel_spmd(nc, [arrays], core_ids=[0]).results[0]["out_x"]
```
